# Optimizing a Trainium2 kernel written in Bass

```python
import numpy as np
import jax
import jax.numpy as jnp

def _softmax(x, axis=-1):
    return jax.nn.softmax(x, axis=axis)
def _gelu(x):
    return jax.nn.gelu(x, approximate=True)
def _silu(x):
    return jax.nn.silu(x)
def _sigmoid(x):
    return jax.nn.sigmoid(x)
def _layernorm(x, axis=-1, eps=1e-5):
    m = jnp.mean(x, axis=axis, keepdims=True)
    v = jnp.var(x, axis=axis, keepdims=True)
    return (x - m) / jnp.sqrt(v + eps)
def _scatter_add(tgt, idx, src, axis=0):
    return tgt.at[idx].add(src)
def _segment_sum(src, seg, n):
    return jax.ops.segment_sum(src, seg, n)

kernel_name = 'mk_conv_seq_d2_conv_nchw256_258f44'

def setup_inputs(seed: int = 0):
    np.random.seed(seed)
    _w = jnp.asarray
    def _rec_inputs():
        import jax
        import jax.numpy as jnp
        _gk = jax.random.key(seed)
        x = -0.0002928 + 1 * jax.random.normal(jax.random.fold_in(_gk, 1), (4, 256, 64, 64), jnp.float32)
        return x
    x = _rec_inputs()
    def _L0_conv_setup():
        import jax, jax.numpy as jnp
        import numpy as np
        B, C, CI, H, W = (4, 256, 128, 64, 64)
        BN_EPS = 1e-05
        key = jax.random.key(seed)
        ks = jax.random.split(key, 11)
        s_in = 1.0 / np.sqrt(C)
        s_mid = 1.0 / np.sqrt(CI)
        return {'x': jax.random.normal(ks[0], (B, C, H, W), jnp.float32), 'theta_w': jax.random.normal(ks[1], (CI, C), jnp.float32) * s_in, 'theta_b': jax.random.normal(ks[2], (CI,), jnp.float32) * s_in, 'phi_w': jax.random.normal(ks[3], (CI, C), jnp.float32) * s_in, 'phi_b': jax.random.normal(ks[4], (CI,), jnp.float32) * s_in, 'g_w': jax.random.normal(ks[5], (CI, C), jnp.float32) * s_in, 'g_b': jax.random.normal(ks[6], (CI,), jnp.float32) * s_in, 'w_w': jax.random.normal(ks[7], (C, CI), jnp.float32) * s_mid, 'w_b': jax.random.normal(ks[8], (C,), jnp.float32) * s_mid, 'gamma': jax.random.normal(ks[9], (C,), jnp.float32) * 0.1 + 1.0, 'beta': jax.random.normal(ks[10], (C,), jnp.float32) * 0.1}
    _L0_conv_all = _L0_conv_setup()
    _L0_conv_in = {k: v for k, v in _L0_conv_all.items() if k in ('theta_w', 'theta_b', 'phi_w', 'phi_b', 'g_w', 'g_b', 'w_w', 'w_b', 'gamma', 'beta', )}
    del _L0_conv_all

    def _L1_conv_setup():
        import jax, jax.numpy as jnp
        import numpy as np
        B, C, H, W = (8, 256, 64, 64)

        def conv1x1(x, w, b):
            return jnp.einsum('oc,nchw->nohw', w, x) + b[None, :, None, None]

        def maxpool2(x):
            return jax.lax.reduce_window(x, -jnp.inf, jax.lax.max, (1, 1, 2, 2), (1, 1, 2, 2), 'VALID')
        key = jax.random.key(seed)
        ks = jax.random.split(key, 10)
        d = C // 8
        dv = C // 2
        s = 0.05
        return {'x': jax.random.normal(ks[0], (B, C, H, W), jnp.float32), 'theta_w': jax.random.normal(ks[1], (d, C), jnp.float32) * s, 'theta_b': jax.random.normal(ks[2], (d,), jnp.float32) * s, 'phi_w': jax.random.normal(ks[3], (d, C), jnp.float32) * s, 'phi_b': jax.random.normal(ks[4], (d,), jnp.float32) * s, 'g_w': jax.random.normal(ks[5], (dv, C), jnp.float32) * s, 'g_b': jax.random.normal(ks[6], (dv,), jnp.float32) * s, 'out_w': jax.random.normal(ks[7], (C, dv), jnp.float32) * s, 'out_b': jax.random.normal(ks[8], (C,), jnp.float32) * s, 'gamma': jnp.array([0.3], jnp.float32)}
    _L1_conv_all = _L1_conv_setup()
    _L1_conv_in = {k: v for k, v in _L1_conv_all.items() if k in ('theta_w', 'theta_b', 'phi_w', 'phi_b', 'g_w', 'g_b', 'out_w', 'out_b', 'gamma', )}
    del _L1_conv_all

    return {
        "x": x,
        "L0_conv_theta_w": _L0_conv_in["theta_w"],
        "L0_conv_theta_b": _L0_conv_in["theta_b"],
        "L0_conv_phi_w": _L0_conv_in["phi_w"],
        "L0_conv_phi_b": _L0_conv_in["phi_b"],
        "L0_conv_g_w": _L0_conv_in["g_w"],
        "L0_conv_g_b": _L0_conv_in["g_b"],
        "L0_conv_w_w": _L0_conv_in["w_w"],
        "L0_conv_w_b": _L0_conv_in["w_b"],
        "L0_conv_gamma": _L0_conv_in["gamma"],
        "L0_conv_beta": _L0_conv_in["beta"],
        "L1_conv_theta_w": _L1_conv_in["theta_w"],
        "L1_conv_theta_b": _L1_conv_in["theta_b"],
        "L1_conv_phi_w": _L1_conv_in["phi_w"],
        "L1_conv_phi_b": _L1_conv_in["phi_b"],
        "L1_conv_g_w": _L1_conv_in["g_w"],
        "L1_conv_g_b": _L1_conv_in["g_b"],
        "L1_conv_out_w": _L1_conv_in["out_w"],
        "L1_conv_out_b": _L1_conv_in["out_b"],
        "L1_conv_gamma": _L1_conv_in["gamma"],
    }

def reference(x, L0_conv_theta_w, L0_conv_theta_b, L0_conv_phi_w, L0_conv_phi_b, L0_conv_g_w, L0_conv_g_b, L0_conv_w_w, L0_conv_w_b, L0_conv_gamma, L0_conv_beta, L1_conv_theta_w, L1_conv_theta_b, L1_conv_phi_w, L1_conv_phi_b, L1_conv_g_w, L1_conv_g_b, L1_conv_out_w, L1_conv_out_b, L1_conv_gamma):
    import jax
    import jax.numpy as jnp
    def _L0_conv_ref(x, theta_w, theta_b, phi_w, phi_b, g_w, g_b, w_w, w_b, gamma, beta):
        import jax, jax.numpy as jnp
        import numpy as np
        B, C, CI, H, W = (4, 256, 128, 64, 64)
        BN_EPS = 1e-05
        b, c, h, w = x.shape
        n = h * w
        xf = x.reshape(b, c, n)
        theta_x = jnp.einsum('ic,bcn->bni', theta_w, xf) + theta_b
        phi_x = jnp.einsum('ic,bcn->bin', phi_w, xf) + phi_b[None, :, None]
        g_x = jnp.einsum('ic,bcn->bni', g_w, xf) + g_b
        f = jnp.einsum('bni,bim->bnm', theta_x, phi_x) / n
        y = jnp.einsum('bnm,bmi->bni', f, g_x)
        y = y.transpose(0, 2, 1).reshape(b, theta_w.shape[0], h, w)
        wy = jnp.einsum('ci,bihw->bchw', w_w, y) + w_b[None, :, None, None]
        mean = jnp.mean(wy, axis=(0, 2, 3), keepdims=True)
        var = jnp.var(wy, axis=(0, 2, 3), keepdims=True)
        wy_bn = (wy - mean) * jax.lax.rsqrt(var + BN_EPS)
        wy_bn = wy_bn * gamma[None, :, None, None] + beta[None, :, None, None]
        return wy_bn + x

    def _L1_conv_ref(x, theta_w, theta_b, phi_w, phi_b, g_w, g_b, out_w, out_b, gamma):
        import jax, jax.numpy as jnp
        import numpy as np
        B, C, H, W = (8, 256, 64, 64)

        def conv1x1(x, w, b):
            return jnp.einsum('oc,nchw->nohw', w, x) + b[None, :, None, None]

        def maxpool2(x):
            return jax.lax.reduce_window(x, -jnp.inf, jax.lax.max, (1, 1, 2, 2), (1, 1, 2, 2), 'VALID')
        n, c, h, w = x.shape
        N, M = (h * w, h // 2 * (w // 2))
        theta = conv1x1(x, theta_w, theta_b).reshape(n, c // 8, N).transpose(0, 2, 1)
        phi = maxpool2(conv1x1(x, phi_w, phi_b)).reshape(n, c // 8, M)
        energy = jnp.einsum('nid,ndj->nij', theta, phi)
        attention = jax.nn.softmax(energy, axis=-1)
        g = maxpool2(conv1x1(x, g_w, g_b)).reshape(n, c // 2, M)
        out = jnp.einsum('ncj,nij->nci', g, attention)
        out = out.reshape(n, c // 2, h, w)
        out = conv1x1(out, out_w, out_b)
        return gamma * out + x

    def _gn(v, G=32, eps=1e-5):
        B_, C_, H_, W_ = v.shape
        g = v.reshape(B_, G, C_ // G, H_, W_)
        m = jnp.mean(g, axis=(2, 3, 4), keepdims=True)
        s = jnp.var(g, axis=(2, 3, 4), keepdims=True)
        return ((g - m) / jnp.sqrt(s + eps)).reshape(v.shape)

    def _ln_c(v, eps=1e-6):
        m = jnp.mean(v, axis=1, keepdims=True)
        s = jnp.var(v, axis=1, keepdims=True)
        return (v - m) / jnp.sqrt(s + eps)

    def _ln_t(v, eps=1e-5):
        m = jnp.mean(v, axis=-1, keepdims=True)
        s = jnp.var(v, axis=-1, keepdims=True)
        return (v - m) / jnp.sqrt(s + eps)

    def _to_tokens(v):
        B_, C_, H_, W_ = v.shape
        return v.reshape(B_, C_, H_ * W_).transpose(0, 2, 1)
    def _from_tokens(t, like):
        B_, C_, H_, W_ = like.shape
        return t.transpose(0, 2, 1).reshape(B_, C_, H_, W_)

    x = _L0_conv_ref(x, L0_conv_theta_w, L0_conv_theta_b, L0_conv_phi_w, L0_conv_phi_b, L0_conv_g_w, L0_conv_g_b, L0_conv_w_w, L0_conv_w_b, L0_conv_gamma, L0_conv_beta)
    x = _L1_conv_ref(x, L1_conv_theta_w, L1_conv_theta_b, L1_conv_phi_w, L1_conv_phi_b, L1_conv_g_w, L1_conv_g_b, L1_conv_out_w, L1_conv_out_b, L1_conv_gamma)
    return x


_drawn_inputs = setup_inputs


def setup_inputs(seed=0):
    import zlib

    import numpy as np

    out = dict(_drawn_inputs(seed))
    spreads = {}
    factors = {'L0_conv_theta_b': 6.361,
     'L0_conv_w_b': 8.0,
     'L1_conv_theta_b': 8.0,
     'L1_conv_phi_b': 8.0,
     'L1_conv_g_b': 8.0,
     'L1_conv_out_b': 5.643}
    for name, (base, spread) in spreads.items():
        noise = np.random.default_rng([zlib.crc32(name.encode()), seed]).standard_normal(out[name].shape)
        drawn = base * np.exp(spread * noise) if base else spread * noise
        out[name] = jnp.asarray(drawn.astype(out[name].dtype))
    for name, factor in factors.items():
        out[name] = (out[name] * factor).astype(out[name].dtype)
    return out
```

```python
from contextlib import ExitStack

import concourse.bass as bass
from concourse import mybir

F32 = mybir.dt.float32
F32R = mybir.dt.float32r
ALU = mybir.AluOpType
ACT = mybir.ActivationFunctionType
AX = mybir.AxisListType

P = 128
B, C, HW = 4, 256, 4096
W_IMG = 64
KT = C // P
CH = 512
NC = HW // CH
NP = B * NC
TL = CH // P
J = HW // 4
JC = J // P
D = C // 8
DV = C // 2
PCH = CH // 4
NS = NP * TL
LEAD = 10
BN_EPS = 1e-5

XRING = 8
X1RING = 16
GPRING = 4
O_ACC, O_S1, O_HL = 8192, 12288, 14336
O_C, O_T1, O_MN, O_V, O_A, O_AT, O_JUNK = 0, 2048, 3072, 3584, 4624, 6704, 9000
O_WPG, O_WT, O_WW, O_W1, O_WTT, O_EYE, O_WO, O_ROWS, O_RB, O_GWO = \
    0, 512, 768, 1024, 1408, 1664, 2176, 2432, 2688, 5760
W_AH, W_AL, W_TA, W_TB, W_GH, W_GL, W_SET = 0, 512, 1024, 1280, 1536, 1792, 2048
S_M, S_TB, S_Q, S_WB, S_CB, S_MU, S_DEV, S_VAR, S_S, S_D, S_FB, S_BT, S_BG, S_GB, S_RT, S_W = \
    0, 8, 16, 24, 32, 40, 42, 50, 52, 54, 62, 70, 74, 78, 80, 82
V_BT, V_WB, V_GAM, V_BETA, V_BO, V_BTP, V_BG, V_G, V_W = 0, 1, 3, 5, 7, 9, 10, 11, 12


def nonlocal_then_attention(nc, x, wpgT, wt, wtT, wwT, w1T, woT, cols, rows, eye, out):
    with ExitStack() as ctx:
        def sb(name, shape, dt=F32):
            return ctx.enter_context(nc.sbuf_tensor(name, shape, dt))

        def sem(name):
            return ctx.enter_context(nc.semaphore(name))

        x1f = sb("x1f", [P, X1RING * KT * CH])
        x1 = x1f[:, :].rearrange("p (s k n) -> p s k n", s=X1RING, k=KT)
        xstage = sb("xstage", [P, 2, KT, CH])
        xsf = sb("xsf", [P, 2 * 2 * KT * CH], F32R)
        xs = xsf[:, :].rearrange("p (a h k n) -> p a h k n", a=2, h=2, k=KT)
        xT = xsf[:, :].rearrange("p (a t h c) -> p a t h c", a=2, t=TL, h=2)
        pf = sb("pf", [P, 2 * TL * J])
        prob = pf[:, :].rearrange("p (a t j) -> p a t j", a=2, t=TL)
        ptf = sb("ptf", [P, 2 * 2 * 2 * CH], F32R)
        pT = ptf[:, :].rearrange("p (a h j n) -> p a h j n", a=2, h=2, j=2)
        theta4 = sb("theta4", [P, 2, CH], F32R)
        phi4 = sb("phi4", [P, 2, J], F32R)
        gpool = sb("gpool", [P, GPRING, PCH])
        graw = sb("graw", [P, PCH])
        gT = sb("gT", [P, 2, 2, JC, DV], F32R)
        tp = sb("tp", [2 * D, CH])
        phip = sb("phip", [2 * D, PCH])
        tph = sb("tph", [2 * D, CH], F32R)
        tpl = sb("tpl", [2 * D, CH], F32R)
        phh = sb("phh", [2 * D, PCH], F32R)
        phl = sb("phl", [2 * D, PCH], F32R)
        oh = sb("oh", [P, CH], F32R)
        ol = sb("ol", [P, CH], F32R)
        ostage = sb("ostage", [P, KT, CH])
        wset = sb("wset", [P, 2, W_SET], F32R)
        woh = sb("woh", [P, C], F32R)
        wol = sb("wol", [P, C], F32R)
        ident = sb("ident", [P, P])
        sm = sb("sm", [P, S_W])
        vc = sb("vc", [P, V_W])
        nmax = sb("nmax", [P, 4])
        den = sb("den", [P, 4])
        rden = sb("rden", [P, 4])

        psum = ctx.enter_context(nc.psum_tensor("psum", [P, 8, 512], F32))
        B_T, B_E, B_O, B_X1, B_TG, B_Y = 0, 2, 4, 5, 6, 7

        scr_theta = nc.dram_tensor("scr_theta", [NP, 2 * D, CH], F32)
        scr_phi = nc.dram_tensor("scr_phi", [B, 2, D, J], F32)
        scr_w = nc.dram_tensor("scr_w", [2, P, W_SET], F32)

        xin = [sem(f"xin{i}") for i in range(XRING)]
        consts = sem("consts")
        tr_mm = sem("tr_mm")
        tr_hi = sem("tr_hi")
        tr_lo = sem("tr_lo")
        acc_done = sem("acc_done")
        gram_mm = sem("gram_mm")
        gram_hl = sem("gram_hl")
        gram_ev = sem("gram_ev")
        mid_mm = sem("mid_mm")
        mid_ev = sem("mid_ev")
        chain = sem("chain")
        means = sem("means")
        variance = sem("variance")
        root = sem("root")
        w_ready = sem("w_ready")
        w_saved = sem("w_saved")
        w_back = sem("w_back")
        xst = [sem(f"xst{i}") for i in range(2)]
        xs_hi = sem("xs_hi")
        xs_lo = sem("xs_lo")
        x1_mm = sem("x1_mm")
        x1_ev = sem("x1_ev")
        th_mm = sem("th_mm")
        th_half = sem("th_half")
        th_sum = sem("th_sum")
        phi_pool = sem("phi_pool")
        phi_hi = sem("phi_hi")
        phi_lo = sem("phi_lo")
        th_hi = sem("th_hi")
        th_lo = sem("th_lo")
        tp_saved = sem("tp_saved")
        g_mm = sem("g_mm")
        g_raw = sem("g_raw")
        g_bias = sem("g_bias")
        gt_mm = sem("gt_mm")
        gt_hi = sem("gt_hi")
        gt_lo = sem("gt_lo")
        th4 = [sem(f"th4_{i}") for i in range(2)]
        ph4 = sem("ph4")
        e_mm = sem("e_mm")
        mx = sem("mx")
        ex = sem("ex")
        rd = sem("rd")
        nrm = sem("nrm")
        pt_mm = sem("pt_mm")
        pt_hi = sem("pt_hi")
        pt_lo = sem("pt_lo")
        pv_mm = sem("pv_mm")
        o_hi = sem("o_hi")
        o_lo = sem("o_lo")
        y_mm = sem("y_mm")
        y_ev = sem("y_ev")
        stored = sem("stored")

        x_v = x.rearrange("b (k p) n -> b p k n", p=P)
        out_v = out.rearrange("b (k p) n -> b p k n", p=P)

        def mid(off, b, n):
            return x1f[:, off + b * n:off + b * n + n]

        def cst(off, n, parts=P):
            return pf[0:parts, off:off + n]

        wpg_s = cst(O_WPG, 512).rearrange("p (k n) -> p k n", k=KT)
        w1_s = cst(O_W1, KT * 192).rearrange("p (k n) -> p k n", k=KT)
        wtT_s = cst(O_WTT, 256).rearrange("p (k n) -> p k n", k=KT)
        eye_s = cst(O_EYE, 512).rearrange("p (k n) -> p k n", k=KT)
        wt_s, ww_s, wo_s = cst(O_WT, 256), cst(O_WW, 256), cst(O_WO, 256)

        def rowbuf(b, part):
            return pf[0:1, O_RB + b * 768 + part * 256:O_RB + b * 768 + part * 256 + 256]

        def acc(b):
            return mid(O_ACC, b, 1024).rearrange("p (k n) -> p k n", k=KT)

        def kk(ap):
            return ap.rearrange("p (k n) -> p k n", k=KT)

        def wmid(b, off, n):
            if b < 2:
                return wset[:, b, off:off + n]
            return ptf[:, (b - 2) * W_SET + off:(b - 2) * W_SET + off + n]

        N_CONST = 10
        MID_STATS = 9 * B
        MID_ALL = 12 * B
        block = ctx.enter_context(nc.Block())

        @block.sync
        def _(sp):
            for n in range(NP):
                if n >= XRING:
                    sp.wait_ge(tr_mm, n - XRING + 1)
                    sp.wait_ge(acc_done, n - XRING + 1)
                b, c = divmod(n, NC)
                sp.dma_start(x1[:, n % XRING], x_v[b, :, :, c * CH:(c + 1) * CH]).then_inc(xin[n % XRING], 16)

            def load_x(p):
                b, c = divmod(p, NC)
                if p >= 2:
                    sp.wait_ge(xs_lo, p - 1)
                sp.dma_start(xstage[:, p % 2], x_v[b, :, :, c * CH:(c + 1) * CH]).then_inc(xst[p % 2], 16)

            def save_tp(p):
                b, c = divmod(p, NC)
                sp.wait_ge(th_lo, p + 1)
                sp.dma_start(scr_theta[p, 0:D], tph[0:D].bitcast(F32)).then_inc(tp_saved, 16)
                sp.dma_start(scr_theta[p, D:2 * D], tpl[0:D].bitcast(F32)).then_inc(tp_saved, 16)
                sp.wait_ge(phi_lo, p + 1)
                sp.dma_start(scr_phi[b, 0, :, c * PCH:(c + 1) * PCH], phh[D:2 * D].bitcast(F32)).then_inc(tp_saved, 16)
                sp.dma_start(scr_phi[b, 1, :, c * PCH:(c + 1) * PCH], phl[D:2 * D].bitcast(F32)).then_inc(tp_saved, 16)

            def load_theta(m):
                if m >= 2:
                    sp.wait_ge(e_mm, TL * (m - 1))
                sp.wait_ge(tp_saved, 64 * (m + 1))
                for h in range(2):
                    sp.dma_start(theta4[2 * D * h:2 * D * (h + 1), m % 2].bitcast(F32), scr_theta[m]).then_inc(th4[m % 2], 16)

            def load_phi(b):
                sp.wait_ge(tp_saved, 64 * NC * (b + 1))
                if b >= 2:
                    sp.wait_ge(e_mm, TL * NC * (b - 1))
                for q in range(4):
                    sp.dma_start(phi4[D * q:D * (q + 1), b % 2].bitcast(F32), scr_phi[b, q // 2]).then_inc(ph4, 16)

            load_x(0)
            load_x(1)
            sp.wait_ge(mid_ev, MID_ALL)
            sp.dma_start(scr_w.rearrange("a p n -> p a n"), ptf[:, :].bitcast(F32).rearrange("p (a n) -> p a n", a=2)).then_inc(w_saved, 16)
            for p in range(LEAD):
                load_x(p + 2)
                save_tp(p)
            load_phi(0)
            load_theta(0)
            load_theta(1)
            for t in range(NP + 1):
                p = t + LEAD
                if p + 2 < NP:
                    load_x(p + 2)
                for b in (2, 3):
                    if p == NC * (b - 1) + (2 if b == 2 else 0):
                        sp.wait_ge(w_saved, 16)
                        sp.wait_ge(g_mm, NC * (b - 1))
                        sp.wait_ge(x1_mm, KT * NC * (b - 1))
                        sp.dma_start(wset[:, b % 2].bitcast(F32), scr_w[b - 2]).then_inc(w_back, 16)
                if t + 2 < NP:
                    if (t + 2) % NC == 0:
                        load_phi((t + 2) // NC)
                    load_theta(t + 2)
                if p < NP:
                    save_tp(p)
                if t >= 1:
                    b, c = divmod(t - 1, NC)
                    sp.wait_ge(y_ev, KT * t)
                    sp.dma_start(out_v[b, :, :, c * CH:(c + 1) * CH], ostage[:]).then_inc(stored, 16)
            sp.wait_ge(stored, 16 * NP)

        @block.gpsimd
        def _(pool):
            for n in range(NP):
                b, c = divmod(n, NC)
                if c == 1:
                    pool.wait_ge(xin[(n - 1) % XRING], 16 * ((n - 1) // XRING + 1))
                    pool.wait_ge(xin[n % XRING], 16 * (n // XRING + 1))
                    nc.gpsimd.tensor_tensor(acc(b), x1[:, (n - 1) % XRING], x1[:, n % XRING], ALU.add).then_inc(acc_done, 2)
                elif c > 1:
                    pool.wait_ge(xin[n % XRING], 16 * (n // XRING + 1))
                    pool.wait_ge(acc_done, n)
                    nc.gpsimd.tensor_tensor(acc(b), acc(b), x1[:, n % XRING], ALU.add).then_inc(acc_done, 1)

            def split_hi(p):
                pool.wait_ge(xst[p % 2], 16 * (p // 2 + 1))
                if p >= 2:
                    pool.wait_ge(g_mm, p - 1)
                    pool.wait_ge(x1_mm, KT * (p - 1))
                else:
                    pool.wait_ge(gram_mm, NP)
                nc.gpsimd.tensor_copy(xs[:, p % 2, 0], xstage[:, p % 2]).then_inc(xs_hi, 1)

            def split_lo(p):
                pool.wait_ge(xs_hi, p + 1)
                nc.gpsimd.tensor_tensor(xs[:, p % 2, 1], xstage[:, p % 2], xs[:, p % 2, 0], ALU.subtract).then_inc(xs_lo, 1)

            def split_theta(p):
                pool.wait_ge(th_sum, p + 1)
                if p >= 1:
                    pool.wait_ge(tp_saved, 64 * p)
                nc.gpsimd.tensor_copy(tph[0:D], tp[0:D]).then_inc(th_hi, 1)
                pool.wait_ge(th_hi, p + 1)
                nc.gpsimd.tensor_tensor(tpl[0:D], tp[0:D], tph[0:D], ALU.subtract).then_inc(th_lo, 1)

            def bias_g(p):
                pool.wait_ge(g_raw, p + 1)
                if p >= GPRING:
                    pool.wait_ge(gt_mm, p - GPRING + 1)
                b = p // NC
                nc.gpsimd.tensor_scalar(gpool[:, p % GPRING], graw[:], sm[:, S_BG + b:S_BG + b + 1], None, ALU.add).then_inc(g_bias, 1)

            def normalise(e):
                pool.wait_ge(rd, e + 1)
                pr = prob[:, (e // TL) % 2, e % TL]
                nc.gpsimd.tensor_scalar(pr, pr, rden[:, e % 4:e % 4 + 1], 1.0, ALU.mult, ALU.mult).then_inc(nrm, 1)

            split_hi(0)
            split_lo(0)
            for p in range(LEAD):
                split_hi(p + 1)
                split_lo(p + 1)
                split_theta(p)
                bias_g(p)
            for e in range(4):
                normalise(e)
            for s in range(NS):
                t, q = divmod(s, TL)
                p = t + LEAD
                if s + 4 < NS:
                    normalise(s + 4)
                if q == 0 and p + 1 < NP:
                    split_hi(p + 1)
                if q == 1 and p + 1 < NP:
                    split_lo(p + 1)
                if q == 2 and p < NP:
                    split_theta(p)
                if q == 3 and p < NP:
                    bias_g(p)

        @block.scalar
        def _(act):
            for dst, src in ((ident[:], eye[:, 0:P]), (cst(O_WPG, 512), wpgT), (cst(O_WT, 256), wt),
                             (cst(O_WTT, 256), wtT), (cst(O_WW, 256), wwT), (cst(O_W1, KT * 192), w1T),
                             (cst(O_WO, 256), woT), (cst(O_EYE, 512), eye), (vc[:], cols),
                             (cst(O_ROWS, 256, 1), rows)):
                act.dma_start(dst, src).then_inc(consts, 16)

            def gram_out(b):
                act.wait_ge(gram_mm, NC * (b + 1))
                for m in range(KT):
                    ins = nc.scalar.activation(kk(mid(O_HL, b, 512))[:, m], psum[:, 4 + 2 * (b % 2) + m, 256:512],
                                               ACT.Copy, scale=1.0 / HW)
                ins.then_inc(gram_hl, 1)

            for n in range(NP):
                act.wait_ge(tr_mm, n + 1)
                if n >= 2:
                    act.wait_ge(gram_mm, n - 1)
                nc.scalar.copy(xT[:, n % 2, :, 0], psum[:, 2 * (n % 2):2 * (n % 2) + 2].rearrange("p a (t c) -> p (a t) c", c=C)).then_inc(tr_hi, 1)
                if n % NC == 1 and n > NC:
                    gram_out(n // NC - 1)
            gram_out(B - 1)
            act.wait_ge(variance, 1)
            nc.scalar.activation(sm[:, S_RT:S_RT + 2], sm[:, S_VAR:S_VAR + 2], ACT.Sqrt).then_inc(root, 1)

            def x1_out(p, m):
                b = p // NC
                act.wait_ge(x1_mm, KT * p + m + 1)
                if p >= X1RING:
                    act.wait_ge(y_ev, KT * (p - X1RING) + KT)
                elif p == 0:
                    act.wait_ge(mid_ev, MID_ALL)
                nc.scalar.activation(x1[:, p % X1RING, m], psum[:, B_X1], ACT.Identity,
                                     bias=sm[:, S_FB + 2 * b + m:S_FB + 2 * b + m + 1]).then_inc(x1_ev, 1)

            def theta_out(p):
                b = p // NC
                act.wait_ge(th_mm, p + 1)
                if p >= 1:
                    act.wait_ge(th_lo, p)
                    act.wait_ge(phi_pool, p)
                nc.scalar.activation(tp[:], psum[0:2 * D, B_TG], ACT.Identity,
                                     bias=sm[0:2 * D, S_BT + b:S_BT + b + 1]).then_inc(th_half, 1)

            def exponent(e):
                act.wait_ge(mx, e + 1)
                m, r = divmod(e, TL)
                if e == 0:
                    act.wait_ge(mid_ev, MID_ALL)
                if e >= 2 * TL:
                    act.wait_ge(pt_mm, TL * (m - 1))
                if e >= 4:
                    act.wait_ge(rd, e - 3)
                nc.scalar.activation(prob[:, m % 2, r], psum[:, B_E:B_E + 2], ACT.Exp,
                                     bias=nmax[:, e % 4:e % 4 + 1], accum_out=den[:, e % 4:e % 4 + 1]).then_inc(ex, 1)

            def probs_hi(s):
                act.wait_ge(pt_mm, s + 1)
                if s >= 2:
                    act.wait_ge(pv_mm, s - 1)
                if s == 0:
                    act.wait_ge(w_saved, 16)
                nc.scalar.copy(pT[:, s % 2, 0], psum[:, B_T:B_T + 2]).then_inc(pt_hi, 1)

            def attn_hi(t):
                act.wait_ge(pv_mm, TL * (t + 1))
                if t >= 1:
                    act.wait_ge(y_mm, KT * t)
                nc.scalar.copy(oh[:], psum[:, B_O]).then_inc(o_hi, 1)

            for p in range(LEAD):
                x1_out(p, 0)
                x1_out(p, 1)
                theta_out(p)
            for e in range(5):
                exponent(e)
            for s in range(NS + 1):
                t, q = divmod(s, TL)
                p = t + LEAD
                if s < NS:
                    probs_hi(s)
                if q == 0 and t >= 1:
                    attn_hi(t - 1)
                if s + 5 < NS:
                    exponent(s + 5)
                if p < NP:
                    if q == 0:
                        x1_out(p, 0)
                    if q == 1:
                        theta_out(p)
                    if q == 3:
                        x1_out(p, 1)

        @block.tensor
        def _(pe):
            def split_product(o, wh, wl, vh, vl, start, stop):
                nc.tensor.matmul(o, wh, vh, start=start, stop=False)
                nc.tensor.matmul(o, wl, vh, start=False, stop=False)
                return nc.tensor.matmul(o, wh, vl, start=False, stop=stop)

            def gram(n):
                b, c = divmod(n, NC)
                pe.wait_ge(tr_lo, n + 1)
                if c == 0 and b >= 2:
                    pe.wait_ge(gram_ev, b - 1)
                for t in range(TL):
                    for m in range(KT):
                        ins = nc.tensor.matmul(psum[:, 4 + 2 * (b % 2) + m], xT[:, n % 2, t, 0, m * P:(m + 1) * P],
                                               xT[:, n % 2, t], start=(c == 0 and t == 0), stop=(c == NC - 1 and t == TL - 1))
                ins.then_inc(gram_mm, 1)

            pe.wait_ge(consts, 16 * N_CONST)
            for n in range(NP):
                pe.wait_ge(xin[n % XRING], 16 * (n // XRING + 1))
                if n >= 2:
                    pe.wait_ge(tr_lo, n - 1)
                for t in range(TL):
                    for k in range(KT):
                        ins = nc.tensor.transpose(psum[:, 2 * (n % 2) + t // 2, (t % 2) * C + k * P:(t % 2) * C + (k + 1) * P],
                                                  x1[:, n % XRING, k, t * P:(t + 1) * P], ident[:])
                ins.then_inc(tr_mm, 1)
                if n >= 1:
                    gram(n - 1)
            gram(NP - 1)

            def bank(stage, b):
                return psum[:, (stage % 2) * 4 + b]

            def stage_products(stage):
                for b in range(B):
                    i = stage * B + b
                    o = bank(stage, b)
                    if stage:
                        pe.wait_ge(mid_ev, i - B + 1)
                    if stage == 0:
                        if b == 0:
                            pe.wait_ge(means, 1)
                        mcol = sm[:, S_M + 2 * b:S_M + 2 * b + 2]
                        for k in range(KT):
                            nc.tensor.matmul(o[0:1, k * P:(k + 1) * P], mcol[:, k:k + 1], ident[:], start=True, stop=True)
                        for k in range(KT):
                            nc.tensor.matmul(o[0:1, 256:512], mcol[:, k:k + 1], wpg_s[:, k], start=(k == 0), stop=False)
                        ins = nc.tensor.matmul(o[0:1, 256:512], ident[0:1, 0:1], cst(O_ROWS, 256, 1), start=False, stop=True)
                    elif stage == 1:
                        hl = kk(mid(O_HL, b, 512))
                        for m in range(KT):
                            for k in range(KT):
                                oo = o[:, m * C + k * P:m * C + (k + 1) * P]
                                nc.tensor.matmul(oo, hl[:, k, m * P:(m + 1) * P], ident[:], start=True, stop=False)
                                ins = nc.tensor.matmul(oo, rowbuf(b, 1)[:, m * P:(m + 1) * P], rowbuf(b, 0)[:, k * P:(k + 1) * P],
                                                       start=False, stop=True)
                    elif stage == 2:
                        cv = kk(mid(O_C, b, 512))
                        for m in range(KT):
                            for k in range(KT):
                                nc.tensor.matmul(o[:, m * P:(m + 1) * P], cv[:, k, m * P:(m + 1) * P], wpg_s[:, k, P:2 * P],
                                                 start=(k == 0), stop=(k == 1))
                        for k in range(KT):
                            ins = nc.tensor.matmul(o[:, 256:257], wtT_s[:, k], sm[:, S_M + 2 * b + k:S_M + 2 * b + k + 1],
                                                   start=(k == 0), stop=(k == 1))
                    elif stage == 3:
                        t1 = kk(mid(O_T1, b, 256))
                        for k in range(KT):
                            nc.tensor.matmul(o[:, 0:P], wpg_s[:, k, 0:P], t1[:, k], start=(k == 0), stop=False)
                        ins = nc.tensor.matmul(o[:, 0:P], rowbuf(b, 2)[:, 0:P], rowbuf(b, 2)[:, P:2 * P], start=False, stop=True)
                    elif stage == 4:
                        nc.tensor.matmul(o[:, 0:C], mid(O_MN, b, P), wt_s, start=True, stop=True)
                        ins = nc.tensor.matmul(o[:, C:C + 2], mid(O_MN, b, P), sm[:, S_TB + 2 * b:S_TB + 2 * b + 2], start=True, stop=True)
                    elif stage in (5, 6):
                        m = stage - 5
                        ins = nc.tensor.matmul(o[:, 0:C + 2], ww_s[:, m * P:(m + 1) * P], mid(O_V, b, 260)[:, 0:C + 2], start=True, stop=True)
                    elif stage == 7:
                        for m in range(KT):
                            ins = nc.tensor.matmul(o[:, m * C:(m + 1) * C], mid(O_V, b, 260)[:, m * P:(m + 1) * P], ww_s, start=True, stop=True)
                    elif stage == 8:
                        at, cv = kk(mid(O_AT, b, 512)), kk(mid(O_C, b, 512))
                        for m in range(KT):
                            for k in range(KT):
                                ins = nc.tensor.matmul(o[:, m * C:(m + 1) * C], at[:, k, m * P:(m + 1) * P], cv[:, k],
                                                       start=(k == 0), stop=(k == 1))
                    elif stage == 9:
                        if b == 0:
                            pe.wait_ge(w_ready, 1)
                        a = kk(mid(O_A, b, 520))
                        for ck in range(KT):
                            for m in range(KT):
                                ins = nc.tensor.transpose(o[:, ck * C + m * P:ck * C + (m + 1) * P], a[:, m, ck * P:(ck + 1) * P], ident[:])
                    elif stage == 10:
                        a = kk(mid(O_A, b, 520))
                        for ck in range(KT):
                            for m in range(KT):
                                ins = nc.tensor.matmul(o[:, ck * 192:(ck + 1) * 192], a[:, m, ck * P:(ck + 1) * P], w1_s[:, m],
                                                       start=(m == 0), stop=(m == 1))
                    else:
                        for m in range(KT):
                            nc.tensor.matmul(o[0:2 * D, 0:1], w1_s[:, m, 0:2 * D], sm[:, S_D + 2 * b + m:S_D + 2 * b + m + 1],
                                             start=(m == 0), stop=(m == 1))
                        for m in range(KT):
                            ins = nc.tensor.matmul(o[:, 1:2], w1_s[:, m, 2 * D:192], sm[:, S_D + 2 * b + m:S_D + 2 * b + m + 1],
                                                   start=(m == 0), stop=(m == 1))
                    ins.then_inc(mid_mm, 1)

            pe.wait_ge(gram_ev, B)
            for stage in range(12):
                stage_products(stage)

            def weights(b, off, k, n):
                return wset[:, b % 2, off + k * n:off + (k + 1) * n]

            def project_x1(p, m):
                b = p // NC
                if m == 0:
                    pe.wait_ge(xs_lo, p + 1)
                    if p == 0:
                        pe.wait_ge(mid_ev, MID_ALL)
                    if b >= 2 and p % NC == 0:
                        pe.wait_ge(w_back, 16 * (b - 1))
                if KT * p + m >= 1:
                    pe.wait_ge(x1_ev, KT * p + m)
                for k in range(KT):
                    ins = split_product(psum[:, B_X1], weights(b, W_AH, k, C)[:, m * P:(m + 1) * P],
                                        weights(b, W_AL, k, C)[:, m * P:(m + 1) * P], xs[:, p % 2, 0, k], xs[:, p % 2, 1, k],
                                        k == 0, k == KT - 1)
                ins.then_inc(x1_mm, 1)

            def project_theta(p):
                b = p // NC
                if p >= 1:
                    pe.wait_ge(g_raw, p)
                for k in range(KT):
                    nc.tensor.matmul(psum[:, B_TG], weights(b, W_TA, k, P), xs[:, p % 2, 0, k], start=(k == 0), stop=False)
                    ins = nc.tensor.matmul(psum[:, B_TG], weights(b, W_TB, k, P), xs[:, p % 2, 1, k], start=False, stop=(k == KT - 1))
                ins.then_inc(th_mm, 1)

            def project_g(p):
                b = p // NC
                pe.wait_ge(th_sum, p + 1)
                for k in range(KT):
                    ins = split_product(psum[:, B_TG], weights(b, W_GH, k, P), weights(b, W_GL, k, P),
                                        xs[:, p % 2, 0, k], xs[:, p % 2, 1, k], k == 0, k == KT - 1)
                ins.then_inc(g_mm, 1)

            def turn_g(p, outs):
                pe.wait_ge(g_bias, p + 1)
                if p >= 1:
                    pe.wait_ge(gt_lo, p)
                if outs > 0:
                    pe.wait_ge(y_ev, outs)
                nc.tensor.transpose(psum[:, B_Y, 0:P], gpool[:, p % GPRING], ident[:]).then_inc(gt_mm, 1)

            def energies(e):
                m, r = divmod(e, TL)
                b = m // NC
                if r == 0:
                    pe.wait_ge(th4[m % 2], 32 * (m // 2 + 1))
                    if m % NC == 0:
                        pe.wait_ge(ph4, 64 * (b + 1))
                if e >= 1:
                    pe.wait_ge(ex, e)
                for h in range(2):
                    ins = nc.tensor.matmul(psum[:, B_E + h], theta4[:, m % 2, r * P:(r + 1) * P],
                                           phi4[:, b % 2, h * CH:(h + 1) * CH], start=True, stop=True)
                ins.then_inc(e_mm, 1)

            def turn_probs(s):
                t, q = divmod(s, TL)
                if q == 0:
                    pe.wait_ge(nrm, TL * (t + 1))
                if s >= 1:
                    pe.wait_ge(pt_lo, s)
                for jj in range(2):
                    for r in range(TL):
                        ins = nc.tensor.transpose(psum[:, B_T + jj, r * P:(r + 1) * P],
                                                  prob[:, t % 2, r, (2 * q + jj) * P:(2 * q + jj + 1) * P], ident[:])
                ins.then_inc(pt_mm, 1)

            def attend(s):
                t, q = divmod(s, TL)
                b = t // NC
                pe.wait_ge(pt_lo, s + 1)
                if q == 0:
                    if t >= 1:
                        pe.wait_ge(o_lo, t)
                    if t % NC == 0:
                        pe.wait_ge(gt_lo, NC * (b + 1))
                for jj in range(2):
                    ins = split_product(psum[:, B_O], gT[:, b % 2, 0, 2 * q + jj], gT[:, b % 2, 1, 2 * q + jj],
                                        pT[:, s % 2, 0, jj], pT[:, s % 2, 1, jj],
                                        q == 0 and jj == 0, q == TL - 1 and jj == 1)
                ins.then_inc(pv_mm, 1)

            def convolve(t, m):
                pe.wait_ge(o_lo, t + 1)
                if KT * t + m >= 1:
                    pe.wait_ge(y_ev, KT * t + m)
                turned = min(t + 1 + NC, NP)
                pe.wait_ge(gt_lo, turned)
                split_product(psum[:, B_Y], woh[:, m * P:(m + 1) * P], wol[:, m * P:(m + 1) * P], oh[:], ol[:],
                              True, True).then_inc(y_mm, 1)

            for p in range(LEAD):
                project_x1(p, 0)
                project_theta(p)
                project_x1(p, 1)
                project_g(p)
                if 1 <= p <= NC:
                    turn_g(p - 1, 0)
            for e in range(5):
                energies(e)
            for s in range(NS + TL):
                t, q = divmod(s, TL)
                p = t + LEAD
                if s < NS:
                    turn_probs(s)
                if s + 5 < NS:
                    energies(s + 5)
                if q == 0 and p < NP:
                    project_x1(p, 0)
                if q in (1, 2) and t >= 1:
                    convolve(t - 1, q - 1)
                if 1 <= s <= NS:
                    attend(s - 1)
                if p < NP:
                    if q == 1:
                        project_theta(p)
                    if q == 2:
                        project_g(p)
                    if q == 3:
                        project_x1(p, 1)
                if q == 3 and t + NC < NP:
                    turn_g(t + NC, KT * t)

        @block.vector
        def _(dve):
            for n in range(NP):
                b, c = divmod(n, NC)
                dve.wait_ge(tr_hi, n + 1)
                nc.vector.tensor_tensor(xT[:, n % 2, :, 1], psum[:, 2 * (n % 2):2 * (n % 2) + 2].rearrange("p a (t c) -> p (a t) c", c=C),
                                        xT[:, n % 2, :, 0], ALU.subtract).then_inc(tr_lo, 1)

                def gram_sum(b):
                    dve.wait_ge(gram_hl, b + 1)
                    for m in range(KT):
                        ins = nc.vector.scalar_tensor_tensor(kk(mid(O_S1, b, 512))[:, m], psum[:, 4 + 2 * (b % 2) + m, 0:256], 1.0 / HW,
                                                             kk(mid(O_HL, b, 512))[:, m], ALU.mult, ALU.add)
                    ins.then_inc(gram_ev, 1)
                if c == 2 and b >= 1:
                    gram_sum(b - 1)
            gram_sum(B - 1)

            steps = [0]

            def then(ins):
                steps[0] += 1
                ins.then_inc(chain, 1)
                dve.wait_ge(chain, steps[0])

            tt, ts, stt, cp = nc.vector.tensor_tensor, nc.vector.tensor_scalar, nc.vector.scalar_tensor_tensor, nc.vector.tensor_copy
            dve.wait_ge(consts, 16 * N_CONST)
            dve.wait_ge(acc_done, NP)
            for b in range(B):
                ins = nc.vector.tensor_reduce(sm[:, S_M + 2 * b:S_M + 2 * b + 2], acc(b), AX.X, ALU.add)
            then(ins)
            then(ts(sm[:, S_M:S_M + 2 * B], sm[:, S_M:S_M + 2 * B], 1.0 / HW, None, ALU.mult))
            for b in range(B):
                cp(sm[:, S_TB + 2 * b:S_TB + 2 * b + 1], vc[:, V_BT:V_BT + 1])
            then(ts(cst(O_GWO, C), wo_s, vc[:, V_G:V_G + 1], None, ALU.mult))
            then(cp(woh[:], cst(O_GWO, C)))
            tt(wol[:], cst(O_GWO, C), woh[:], ALU.subtract)
            ts(sm[:, S_GB:S_GB + 2], vc[:, V_BO:V_BO + 2], vc[:, V_G:V_G + 1], None, ALU.mult).then_inc(means, 1)

            def per_image(off, m):
                return sm[:, off:off + 2 * B].rearrange("p (b m) -> p b m", m=2)[:, :, m]

            def stage_out(stage):
                for b in range(B):
                    i = stage * B + b
                    o = psum[:, (stage % 2) * 4 + b]
                    dve.wait_ge(mid_mm, i + 1)
                    if stage == 0:
                        cp(rowbuf(b, 0), o[0:1, 0:256])
                        ts(rowbuf(b, 1), o[0:1, 0:256], -1.0, None, ALU.mult)
                        ins = cp(rowbuf(b, 2), o[0:1, 256:512])
                    elif stage == 1:
                        ins = tt(mid(O_C, b, 512), o, mid(O_S1, b, 512), ALU.add)
                    elif stage == 2:
                        cp(mid(O_T1, b, 256), o[:, 0:256])
                        ins = tt(sm[:, S_TB + 2 * b + 1:S_TB + 2 * b + 2], o[:, 256:257], vc[:, V_BT:V_BT + 1], ALU.add)
                    elif stage == 3:
                        ins = cp(mid(O_MN, b, P), o[:, 0:P])
                    elif stage == 4:
                        ins = cp(mid(O_V, b, 260)[:, 0:C + 2], o[:, 0:C + 2])
                    elif stage in (5, 6):
                        ins = cp(kk(mid(O_A, b, 520))[:, stage - 5, 0:C + 2], o[:, 0:C + 2])
                    elif stage == 7:
                        ins = cp(mid(O_AT, b, 512), o)
                    elif stage == 8:
                        a = kk(mid(O_A, b, 520))
                        for m in range(KT):
                            ins = nc.vector.tensor_tensor_reduce(out=x1f[:, O_JUNK + (2 * b + m) * C:O_JUNK + (2 * b + m + 1) * C], in0=o[:, m * C:(m + 1) * C],
                                                                 in1=a[:, m, 0:C], scale=1.0, scalar=0.0, op0=ALU.mult, op1=ALU.add,
                                                                 accum_out=sm[:, S_Q + 2 * b + m:S_Q + 2 * b + m + 1])
                    elif stage == 9:
                        then(cp(wmid(b, W_AH, 512), o))
                        ins = tt(wmid(b, W_AL, 512), o, wmid(b, W_AH, 512), ALU.subtract)
                    elif stage == 10:
                        w = o[:, 0:2 * 192].rearrange("p (k n) -> p k n", k=KT)
                        ta, tb = kk(wmid(b, W_TA, 256)), kk(wmid(b, W_TB, 256))
                        gh, gl = kk(wmid(b, W_GH, 256)), kk(wmid(b, W_GL, 256))
                        ts(tb[:, :, 0:2 * D], w[:, :, 0:2 * D], 0.0, None, ALU.mult)
                        cp(tb[:, :, 2 * D:4 * D], w[:, :, 0:2 * D])
                        cp(ta[:, :, 0:2 * D], w[:, :, 0:2 * D])
                        then(cp(gh, w[:, :, 2 * D:192]))
                        tt(ta[:, :, 2 * D:4 * D], w[:, :, 0:2 * D], ta[:, :, 0:2 * D], ALU.subtract)
                        ins = tt(gl, w[:, :, 2 * D:192], gh, ALU.subtract)
                    else:
                        tt(sm[0:2 * D, S_BT + b:S_BT + b + 1], o[0:2 * D, 0:1], vc[0:2 * D, V_BTP:V_BTP + 1], ALU.add)
                        ins = tt(sm[:, S_BG + b:S_BG + b + 1], o[:, 1:2], vc[:, V_BG:V_BG + 1], ALU.add)
                    ins.then_inc(mid_ev, 1)

            for stage in range(9):
                stage_out(stage)
            dve.wait_ge(mid_ev, MID_STATS)
            for m in range(KT):
                for b in range(B):
                    a = kk(mid(O_A, b, 520))
                    tt(sm[:, S_WB + 2 * b + m:S_WB + 2 * b + m + 1], a[:, m, C + 1:C + 2], vc[:, V_WB + m:V_WB + m + 1], ALU.add)
                    ins = tt(sm[:, S_CB + 2 * b + m:S_CB + 2 * b + m + 1], a[:, m, C:C + 1], vc[:, V_WB + m:V_WB + m + 1], ALU.add)
            then(ins)
            then(nc.vector.tensor_reduce(sm[:, S_MU:S_MU + 2], sm[:, S_WB:S_WB + 8].rearrange("p (b m) -> p m b", m=2), AX.X, ALU.add))
            then(ts(sm[:, S_MU:S_MU + 2], sm[:, S_MU:S_MU + 2], 1.0 / B, None, ALU.mult))
            for m in range(KT):
                ins = ts(per_image(S_DEV, m), per_image(S_WB, m), sm[:, S_MU + m:S_MU + m + 1], None, ALU.subtract)
            then(ins)
            then(tt(sm[:, S_DEV:S_DEV + 8], sm[:, S_DEV:S_DEV + 8], sm[:, S_DEV:S_DEV + 8], ALU.mult))
            then(tt(sm[:, S_DEV:S_DEV + 8], sm[:, S_DEV:S_DEV + 8], sm[:, S_Q:S_Q + 8], ALU.add))
            then(nc.vector.tensor_reduce(sm[:, S_VAR:S_VAR + 2], sm[:, S_DEV:S_DEV + 8].rearrange("p (b m) -> p m b", m=2), AX.X, ALU.add))
            then(ts(sm[:, S_VAR:S_VAR + 2], sm[:, S_VAR:S_VAR + 2], 1.0 / B, None, ALU.mult))
            ts(sm[:, S_VAR:S_VAR + 2], sm[:, S_VAR:S_VAR + 2], BN_EPS, None, ALU.add).then_inc(variance, 1)
            dve.wait_ge(root, 1)
            v, r, h = (sm[:, o:o + 2] for o in (S_VAR, S_S, S_DEV))
            then(nc.vector.reciprocal(r, sm[:, S_RT:S_RT + 2]))
            then(tt(h, r, r, ALU.mult))
            then(tt(h, h, v, ALU.mult))
            then(ts(h, h, -0.5, 1.5, ALU.mult, ALU.add))
            then(tt(r, r, h, ALU.mult))
            then(tt(r, r, vc[:, V_GAM:V_GAM + 2], ALU.mult))
            for m in range(KT):
                ins = ts(per_image(S_D, m), per_image(S_CB, m), sm[:, S_MU + m:S_MU + m + 1], sm[:, S_S + m:S_S + m + 1],
                         ALU.subtract, ALU.mult)
            then(ins)
            for m in range(KT):
                ins = ts(per_image(S_D, m), per_image(S_D, m), vc[:, V_BETA + m:V_BETA + m + 1], None, ALU.add)
            then(ins)
            for m in range(KT):
                ts(per_image(S_FB, m), per_image(S_D, m), sm[:, S_GB + m:S_GB + m + 1], None, ALU.add)
            for b in range(B):
                a = kk(mid(O_A, b, 520))
                for m in range(KT):
                    ins = stt(a[:, m, 0:C], a[:, m, 0:C], sm[:, S_S + m:S_S + m + 1], eye_s[:, m], ALU.mult, ALU.add)
            ins.then_inc(w_ready, 1)
            for stage in range(9, 12):
                stage_out(stage)

            def theta_sum(p):
                dve.wait_ge(th_half, p + 1)
                tt(tp[:], psum[2 * D:4 * D, B_TG], tp[:], ALU.add).then_inc(th_sum, 1)

            def phi_out(p):
                dve.wait_ge(th_sum, p + 1)
                if p >= 1:
                    dve.wait_ge(tp_saved, 64 * p)
                nc.vector.tensor_reduce(phip[D:2 * D].rearrange("p (r c) -> p r c", c=W_IMG // 2),
                                        tp[D:2 * D].rearrange("p (r i c j) -> p r c i j", i=2, j=2, c=W_IMG // 2),
                                        AX.XY, ALU.max).then_inc(phi_pool, 1)
                dve.wait_ge(phi_pool, p + 1)
                cp(phh[D:2 * D], phip[D:2 * D]).then_inc(phi_hi, 1)
                dve.wait_ge(phi_hi, p + 1)
                tt(phl[D:2 * D], phip[D:2 * D], phh[D:2 * D], ALU.subtract).then_inc(phi_lo, 1)

            def pool_g(p):
                dve.wait_ge(g_mm, p + 1)
                if p >= 1:
                    dve.wait_ge(g_bias, p)
                nc.vector.tensor_reduce(graw[:].rearrange("p (r c) -> p r c", c=W_IMG // 2),
                                        psum[:, B_TG].rearrange("p (r i c j) -> p r c i j", i=2, j=2, c=W_IMG // 2),
                                        AX.XY, ALU.max).then_inc(g_raw, 1)

            def split_g(p):
                b, c = divmod(p, NC)
                dve.wait_ge(gt_mm, p + 1)
                if b >= 2:
                    dve.wait_ge(pv_mm, TL * NC * (b - 1))
                cp(gT[:, b % 2, 0, c], psum[:, B_Y, 0:P]).then_inc(gt_hi, 1)
                dve.wait_ge(gt_hi, p + 1)
                tt(gT[:, b % 2, 1, c], psum[:, B_Y, 0:P], gT[:, b % 2, 0, c], ALU.subtract).then_inc(gt_lo, 1)

            def row_max(e):
                dve.wait_ge(e_mm, e + 1)
                if e >= 4:
                    dve.wait_ge(ex, e - 3)
                nc.vector.tensor_reduce(nmax[:, e % 4:e % 4 + 1], psum[:, B_E:B_E + 2], AX.XY, ALU.max, negate=True).then_inc(mx, 1)

            def invert(e):
                dve.wait_ge(ex, e + 1)
                if e >= 4:
                    dve.wait_ge(nrm, e - 3)
                nc.vector.reciprocal(rden[:, e % 4:e % 4 + 1], den[:, e % 4:e % 4 + 1]).then_inc(rd, 1)

            def probs_lo(s):
                dve.wait_ge(pt_hi, s + 1)
                tt(pT[:, s % 2, 1], psum[:, B_T:B_T + 2], pT[:, s % 2, 0], ALU.subtract).then_inc(pt_lo, 1)

            def attn_lo(t):
                dve.wait_ge(o_hi, t + 1)
                tt(ol[:], psum[:, B_O], oh[:], ALU.subtract).then_inc(o_lo, 1)

            def add_x1(t, m):
                dve.wait_ge(y_mm, KT * t + m + 1)
                dve.wait_ge(x1_ev, KT * t + m + 1)
                if m == 0 and t >= 1:
                    dve.wait_ge(stored, 16 * t)
                tt(ostage[:, m], psum[:, B_Y], x1[:, t % X1RING, m], ALU.add).then_inc(y_ev, 1)

            for p in range(LEAD):
                theta_sum(p)
                phi_out(p)
                pool_g(p)
                if 1 <= p <= NC:
                    split_g(p - 1)
            for e in range(5):
                row_max(e)
                if e >= 1:
                    invert(e - 1)
            for s in range(NS + TL):
                t, q = divmod(s, TL)
                p = t + LEAD
                if s + 4 < NS:
                    invert(s + 4)
                if s + 5 < NS:
                    row_max(s + 5)
                if s < NS:
                    probs_lo(s)
                if q == 0 and t >= 1:
                    attn_lo(t - 1)
                if q in (1, 2) and t >= 1:
                    add_x1(t - 1, q - 1)
                if p < NP:
                    if q == 1:
                        theta_sum(p)
                        phi_out(p)
                    if q == 2:
                        pool_g(p)
                if q == 3 and t + NC < NP:
                    split_g(t + NC)


def kernel(**inputs):
    import numpy as np
    import concourse.bacc as bacc
    from concourse.bass_utils import run_bass_kernel_spmd

    def a(name):
        return np.asarray(inputs[name])

    def tiles(w):
        return np.ascontiguousarray(w.reshape(KT, P, -1).transpose(1, 0, 2).reshape(P, -1))

    def col(v):
        return tiles(v.reshape(-1, 1)) if v.size == C else v.reshape(-1, 1)

    xin = a("x").reshape(B, C, HW)
    f = xin.dtype
    btp = np.zeros((P, 1), f)
    btp[0:D, 0] = a("L1_conv_theta_b")
    btp[D:2 * D, 0] = a("L1_conv_phi_b")
    arrays = {
        "x": xin,
        "wpgT": tiles(np.concatenate([a("L0_conv_phi_w"), a("L0_conv_g_w")]).T),
        "wt": a("L0_conv_theta_w"),
        "wtT": tiles(a("L0_conv_theta_w").T),
        "wwT": np.ascontiguousarray(a("L0_conv_w_w").T),
        "w1T": tiles(np.concatenate([a("L1_conv_theta_w"), a("L1_conv_phi_w"), a("L1_conv_g_w")]).T),
        "woT": np.ascontiguousarray(a("L1_conv_out_w").T),
        "cols": np.ascontiguousarray(np.concatenate(
            [col(a("L0_conv_theta_b")), col(a("L0_conv_w_b")), col(a("L0_conv_gamma")), col(a("L0_conv_beta")),
             col(a("L1_conv_out_b")), btp, col(a("L1_conv_g_b")), np.repeat(a("L1_conv_gamma").reshape(1, 1), P, 0)], 1)),
        "rows": np.concatenate([a("L0_conv_phi_b"), a("L0_conv_g_b")]).reshape(1, C),
        "eye": tiles(np.eye(C, dtype=f)),
    }
    nc = bacc.Bacc("TRN2", target_bir_lowering=False, num_devices=1)
    args = [nc.dram_tensor("in_" + n, v.shape, mybir.dt.from_np(v.dtype), kind="ExternalInput").ap() for n, v in arrays.items()]
    out = nc.dram_tensor("out_y", (B, C, HW), F32, kind="ExternalOutput").ap()
    nonlocal_then_attention(nc, *args, out)
    r = run_bass_kernel_spmd(nc, [{"in_" + n: np.ascontiguousarray(v) for n, v in arrays.items()}], core_ids=[0])
    return r.results[0]["out_y"].reshape(B, C, 64, 64)
```

```python
from contextlib import ExitStack

import concourse.bass as bass
from concourse import mybir

F32 = mybir.dt.float32
F32R = mybir.dt.float32r
ALU = mybir.AluOpType
ACT = mybir.ActivationFunctionType
AX = mybir.AxisListType

P = 128
B, C, HW = 4, 256, 4096
W_IMG = 64
KT = C // P
CH = 512
NC = HW // CH
NP = B * NC
TL = CH // P
J = HW // 4
JC = J // P
D = C // 8
DV = C // 2
W1 = 2 * D + DV
PCH = CH // 4
NS = NP * TL
LEAD = 11
AHEAD = 2 * TL
LAG = 2
BN_EPS = 1e-5
EXP_LN_SET = 6

XRING = 8
XTR = 4
XSR = LEAD + 2
GPRING = 4
TH4 = 4
O_ACC, O_DACC, O_TSUM, O_S1, O_HL = 12288, 14336, 15360, 15616, 16640
O_E, O_T1, O_GB, O_MN, O_VT, O_EVT, O_F, O_MREP, O_CST = \
    17664, 18176, 18432, 18560, 18688, 18944, 19200, 19328, 19584
O_T32, O_GWO = 12288, 14336
O_WPG, O_WT, O_WTT, O_WWT, O_WW, O_EW, O_WO, O_BGB, O_END = \
    [O_CST + o for o in (0, 512, 768, 1024, 1280, 1536, 2432, 2688, 2816)]
O_V, O_SU, O_SW, O_JUNK = 0, 1040, 1488, 1744
EW = C + W1
XG = C + DV
W_XH, W_XL, W_GH, W_GL, W_TA, W_TB, W_SET = 0, KT * C, 2 * KT * C, 2 * KT * C + KT * DV, 2 * KT * XG, 2 * KT * XG + KT * P, 2 * KT * XG + 2 * KT * P
W_X = W_GH
S_M, S_TB, S_Q, S_CW, S_WB, S_CB, S_MU, S_DEV, S_VAR, S_S, S_D, S_FB, S_BT, S_BG, S_GB, S_RT, S_AM, S_ONE, S_W = \
    0, 8, 16, 24, 40, 48, 56, 58, 66, 68, 70, 78, 86, 90, 94, 96, 98, 106, 107
V_BT, V_WB, V_GAM, V_BETA, V_BO, V_BTP, V_BG, V_G, V_BP, V_W = 0, 1, 3, 5, 7, 9, 10, 11, 12, 13
STAGES = 7


def nonlocal_then_attention(nc, xT_in, x, wpgT, wt, wtT, wwT, ww, ew, woT, bgB, cols, eye, out):
    with ExitStack() as ctx:
        def sb(name, shape, dt=F32):
            return ctx.enter_context(nc.sbuf_tensor(name, shape, dt))

        def sem(name):
            return ctx.enter_context(nc.semaphore(name))

        with nc.sbuf_tensor("first", [P, XSR * 2 * KT * CH], F32) as first:
            pass
        with nc.sbuf_tensor("first_r", [P, XSR * 2 * KT * CH], F32R) as first_r:
            pass
        xs = sb("xs", [P, XSR, 2, KT, CH], F32R)
        xt_in = first[:, 0:XRING * KT * CH].rearrange("p (s t c) -> p s t c", s=XRING, t=TL)
        xstage = sb("xstage", [P, 2, KT, CH])
        ef = sb("ef", [P, 2 * 2 * CH])
        expT = ef[:, :].rearrange("p (a j n) -> p a j n", a=2, j=2)
        ptf = sb("ptf", [P, 2 * 2 * 2 * CH], F32R)
        xT_half = [m.rearrange("p (a t h c) -> p a t h c", a=2, t=TL, h=2)
                   for m in (ptf[:, :], first_r[:, XRING * KT * CH:XRING * KT * CH + 2 * 2 * KT * CH])]
        pT = ptf[:, :].rearrange("p (a h j n) -> p a h j n", a=2, h=2, j=2)
        theta4 = sb("theta4", [P, TH4, CH], F32R)
        phi4 = sb("phi4", [P, 2, J], F32R)
        gpool = sb("gpool", [P, GPRING, PCH])
        graw = sb("graw", [P, PCH])
        gT = sb("gT", [P, 2, 2, JC, DV], F32R)
        tp = sb("tp", [2 * D, CH])
        phip = sb("phip", [2 * D, PCH])
        tph = sb("tph", [2 * D, CH], F32R)
        tpl = sb("tpl", [2 * D, CH], F32R)
        phh = sb("phh", [2 * D, PCH], F32R)
        phl = sb("phl", [2 * D, PCH], F32R)
        oh = sb("oh", [P, CH], F32R)
        ol = sb("ol", [P, CH], F32R)
        ostage = sb("ostage", [P, KT, CH])
        wset = sb("wset", [P, 2, W_SET], F32R)
        woh = sb("woh", [P, C], F32R)
        wol = sb("wol", [P, C], F32R)
        ident = sb("ident", [P, P])
        sm = sb("sm", [P, S_W])
        vc = sb("vc", [P, V_W])
        nmax = sb("nmax", [P, 2, TL])
        den = sb("den", [P, 2, TL])
        lnden = sb("lnden", [P, TL])
        shift = sb("shift", [P, TL])
        shift_r = sb("shift_r", [P, TL], F32R)
        shift2 = sb("shift2", [P, 2, TL])
        shiftT = sb("shiftT", [2 * TL, P])

        psum = ctx.enter_context(nc.psum_tensor("psum", [P, 8, 512], F32))
        B_E2, B_E1, B_O, B_TG, B_Y = 0, 2, 4, 5, 6

        scr_theta = nc.dram_tensor("scr_theta", [NP, 2 * D, CH], F32)
        scr_phi = nc.dram_tensor("scr_phi", [B, 2, D, J], F32)
        scr_shift = nc.dram_tensor("scr_shift", [NP, 2 * TL, P], F32)
        scr_w = nc.dram_tensor("scr_w", [2, P, W_SET], F32)

        xin = [sem(f"xin{i}") for i in range(XRING)]
        consts = sem("consts")
        tr_hi = sem("tr_hi")
        tr_lo = sem("tr_lo")
        acc_done = sem("acc_done")
        dacc = sem("dacc")
        tsum = sem("tsum")
        ones_set = sem("ones_set")
        gram_mm = sem("gram_mm")
        gram_hl = sem("gram_hl")
        gram_ev = sem("gram_ev")
        mid_mm = sem("mid_mm")
        mid_ev = sem("mid_ev")
        chain = sem("chain")
        variance = sem("variance")
        root = sem("root")
        sw_ready = sem("sw_ready")
        su_mm = sem("su_mm")
        su_ev = sem("su_ev")
        bias_mm = sem("bias_mm")
        bias_ev = sem("bias_ev")
        w_mm = sem("w_mm")
        w_sum = sem("w_sum")
        w_hi = sem("w_hi")
        w_lo = sem("w_lo")
        w_saved = sem("w_saved")
        wx_back = sem("wx_back")
        wp_back = sem("wp_back")
        xst = [sem(f"xst{i}") for i in range(2)]
        xs_hi = sem("xs_hi")
        xs_lo = sem("xs_lo")
        xp_mm = sem("xp_mm")
        th_mm = sem("th_mm")
        th_half = sem("th_half")
        th_sum = sem("th_sum")
        phi_pool = sem("phi_pool")
        phi_hi = sem("phi_hi")
        phi_lo = sem("phi_lo")
        th_hi = sem("th_hi")
        th_lo = sem("th_lo")
        tp_saved = sem("tp_saved")
        g_mm = sem("g_mm")
        g_raw = sem("g_raw")
        g_bias = sem("g_bias")
        gt_mm = sem("gt_mm")
        gt_hi = sem("gt_hi")
        gt_lo = sem("gt_lo")
        wo_done = sem("wo_done")
        th4 = [sem(f"th4_{i}") for i in range(TH4)]
        ph4 = sem("ph4")
        one_rows = sem("one_rows")
        e1_mm = sem("e1_mm")
        mx = sem("mx")
        ex1 = sem("ex1")
        ln_done = sem("ln_done")
        sh_all = sem("sh_all")
        sh_hi = sem("sh_hi")
        sh_two = sem("sh_two")
        sh_mm = sem("sh_mm")
        sh_ev = sem("sh_ev")
        sh_saved = sem("sh_saved")
        sh_row = [sem(f"sh_row{i}") for i in range(TH4)]
        e2_mm = sem("e2_mm")
        ex2 = sem("ex2")
        pt_hi = sem("pt_hi")
        pt_lo = sem("pt_lo")
        pv_mm = sem("pv_mm")
        o_hi = sem("o_hi")
        o_lo = sem("o_lo")
        y_mm = sem("y_mm")
        y_ev = sem("y_ev")
        stored = sem("stored")

        x_v = x.rearrange("b (k p) n -> b p k n", p=P)
        xT_v = xT_in.rearrange("b (c p t) k -> b c p t k", c=NC, p=P)
        out_v = out.rearrange("b (k p) n -> b p k n", p=P)

        def mid(off, n):
            return first[:, off:off + n]

        def cst(off, n):
            return first[:, off:off + n]

        def kk(ap):
            return ap.rearrange("p (k n) -> p k n", k=KT)

        wpg_s, wtT_s, ww_s, ew_s = kk(cst(O_WPG, 512)), kk(cst(O_WTT, 256)), kk(cst(O_WW, 256)), kk(cst(O_EW, KT * EW))
        wt_s, wwT_s, wo_s, bgB_s = cst(O_WT, 256), cst(O_WWT, 256), cst(O_WO, 256), cst(O_BGB, P)
        e_s, t1_s, vt_s, evt_s, mrep_s = (kk(mid(o, n)) for o, n in ((O_E, 512), (O_T1, 256), (O_VT, 256), (O_EVT, 256), (O_MREP, 256)))
        gb_s, mn_s, f_s, tsum_s = mid(O_GB, P), mid(O_MN, P), mid(O_F, P), mid(O_TSUM, C)
        su_s, sw_s = ef[:, O_SU:O_SU + EW], kk(ef[:, O_SW:O_SW + C])

        def v_s(b):
            return ef[:, O_V + 260 * b:O_V + 260 * b + C + 2]

        def acc(b):
            return mid(O_ACC + 1024 * (b % 2), 1024).rearrange("p (t c) -> p t c", t=TL)

        dacc_s = mid(O_DACC, 1024).rearrange("p (t c) -> p t c", t=TL)

        def s1_s(b):
            return mid(O_S1 + 512 * (b % 2), 512)

        def hl_s(b):
            return mid(O_HL + 512 * (b % 2), 512)

        def t32(b):
            return mid(O_T32 + KT * EW * (b % 2), KT * EW)

        def xT(n):
            return xT_half[n % XTR // 2][:, n % 2]

        def smc(off, n=1, parts=P):
            return sm[0:parts, off:off + n]

        def wmid(b, off, n):
            if b < 2:
                return wset[:, b, off:off + n]
            return ptf[:, (b - 2) * W_SET + off:(b - 2) * W_SET + off + n]

        const_loads = ((ident[:], eye), (vc[:], cols), (cst(O_WPG, 512), wpgT), (cst(O_WTT, 256), wtT), (cst(O_BGB, P), bgB),
                       (cst(O_WT, 256), wt), (cst(O_WWT, 256), wwT), (cst(O_WW, 256), ww), (cst(O_EW, KT * EW), ew),
                       (cst(O_WO, 256), woT))
        N_CONST = len(const_loads)
        POOL_CHUNKS = (0, 1, 3, 4, 6, 7)
        DVE_CHUNKS = (2, 5)

        def theta_bank(p):
            return B_TG if p >= LEAD else B_O + p % 2

        def g_bank(p):
            return B_TG if p >= LEAD else B_Y

        def turned_g(p):
            return psum[:, B_TG if p >= NC else B_Y + 1, 0:P]

        def turned_shift(m):
            return psum[0:2 * TL, B_TG if m >= 1 else B_Y + 1, 0:P]

        def energy_banks(e):
            o = B_E2 if e < AHEAD - 1 and e % 2 == 1 else B_E1
            return psum[:, o:o + 2]

        block = ctx.enter_context(nc.Block())

        @block.sync
        def _(sp):
            for n in range(NP):
                b, c = divmod(n, NC)
                if n >= XRING:
                    m = n - XRING
                    sp.wait_ge(tr_lo, m + 1)
                    if c in POOL_CHUNKS:
                        sp.wait_ge(acc_done, NC * (m // NC) + c + 1)
                    else:
                        sp.wait_ge(dacc, m // NC + 1)
                sp.dma_start(xt_in[:, n % XRING], xT_v[b, c]).then_inc(xin[n % XRING], 16)
                if n >= 2 and n - 2 < N_CONST:
                    sp.dma_start(*const_loads[n - 2]).then_inc(consts, 16)

            def load_x(p):
                b, c = divmod(p, NC)
                if p >= 2:
                    sp.wait_ge(xs_lo, p - 1)
                sp.dma_start(xstage[:, p % 2], x_v[b, :, :, c * CH:(c + 1) * CH]).then_inc(xst[p % 2], 16)

            def save_tp(p):
                b, c = divmod(p, NC)
                sp.wait_ge(th_lo, p + 1)
                sp.dma_start(scr_theta[p, 0:D], tph[0:D].bitcast(F32)).then_inc(tp_saved, 16)
                sp.dma_start(scr_theta[p, D:2 * D], tpl[0:D].bitcast(F32)).then_inc(tp_saved, 16)
                sp.wait_ge(phi_lo, p + 1)
                sp.dma_start(scr_phi[b, 0, :, c * PCH:(c + 1) * PCH], phh[D:2 * D].bitcast(F32)).then_inc(tp_saved, 16)
                sp.dma_start(scr_phi[b, 1, :, c * PCH:(c + 1) * PCH], phl[D:2 * D].bitcast(F32)).then_inc(tp_saved, 16)

            def load_theta(m):
                if m >= TH4:
                    sp.wait_ge(e2_mm, TL * (m - TH4 + 1))
                sp.wait_ge(tp_saved, 64 * (m + 1))
                sp.dma_start(theta4[0:2 * D, m % TH4].bitcast(F32), scr_theta[m]).then_inc(th4[m % TH4], 16)
                sp.dma_start(theta4[2 * D:3 * D, m % TH4].bitcast(F32), scr_theta[m, 0:D]).then_inc(th4[m % TH4], 16)

            def load_phi(b):
                sp.wait_ge(tp_saved, 64 * NC * (b + 1))
                if b >= 2:
                    sp.wait_ge(e2_mm, TL * NC * (b - 1))
                for q in range(3):
                    sp.dma_start(phi4[D * q:D * (q + 1), b % 2].bitcast(F32), scr_phi[b, q // 2]).then_inc(ph4, 16)

            def row_shift(m):
                sp.wait_ge(sh_ev, m + 1)
                sp.dma_start(scr_shift[m], shiftT[:]).then_inc(sh_saved, 16)
                sp.wait_ge(sh_saved, 16 * (m + 1))
                sp.dma_start(theta4[3 * D:3 * D + 2, m % TH4].bitcast(F32),
                             scr_shift[m].rearrange("(h r) n -> h (r n)", h=2)).then_inc(sh_row[m % TH4], 16)

            load_x(0)
            load_x(1)
            for p in range(LEAD):
                load_x(p + 2)
                if p >= 1:
                    save_tp(p - 1)
                if p == NC:
                    load_phi(0)
                    for m in range(3):
                        load_theta(m)
                if p == 6:
                    sp.wait_ge(w_lo, B)
                    sp.dma_start(scr_w.rearrange("a p n -> p a n"),
                                 ptf[:, 0:2 * W_SET].bitcast(F32).rearrange("p (a n) -> p a n", a=2)).then_inc(w_saved, 16)
            save_tp(LEAD - 1)
            row_shift(0)
            for t in range(NP + 2):
                p = t + LEAD
                if t >= 2:
                    b, c = divmod(t - 2, NC)
                    sp.wait_ge(y_ev, KT * (t - 1))
                    sp.dma_start(out_v[b, :, :, c * CH:(c + 1) * CH], ostage[:]).then_inc(stored, 16)
                if p + 2 < NP:
                    load_x(p + 2)
                if t + 3 < NP:
                    load_theta(t + 3)
                for b in (2, 3):
                    if t == (0 if b == 2 else NC * (b - 1) - LEAD + 1):
                        sp.wait_ge(w_saved, 16)
                        sp.wait_ge(g_mm, NC * (b - 1))
                        sp.dma_start(wset[:, b % 2, W_X:W_SET].bitcast(F32), scr_w[b - 2, :, W_X:W_SET]).then_inc(wp_back, 16)
                    if t == NC * (b - 1) + 1:
                        sp.wait_ge(xp_mm, KT * NC * (b - 1))
                        sp.dma_start(wset[:, b % 2, 0:W_X].bitcast(F32), scr_w[b - 2, :, 0:W_X]).then_inc(wx_back, 16)
                if t + 1 < NP:
                    row_shift(t + 1)
                if 1 <= t and p - 1 < NP:
                    save_tp(p - 1)
                if t + 3 < NP and (t + 3) % NC == 0:
                    load_phi((t + 3) // NC)
            sp.wait_ge(stored, 16 * NP)

        @block.gpsimd
        def _(pool):
            nc.gpsimd.memset(smc(S_ONE), 1.0 / HW).then_inc(ones_set, 1)
            pool.wait_ge(ones_set, 1)
            nc.gpsimd.memset(phi4[3 * D:3 * D + 2].bitcast(F32), 1.0).then_inc(one_rows, 1)
            pool.wait_ge(one_rows, 1)
            for n in range(NP):
                b, c = divmod(n, NC)
                if c == 1:
                    pool.wait_ge(xin[(n - 1) % XRING], 16 * ((n - 1) // XRING + 1))
                    pool.wait_ge(xin[n % XRING], 16 * (n // XRING + 1))
                    if b >= 2:
                        pool.wait_ge(tsum, b - 1)
                    nc.gpsimd.tensor_tensor(acc(b), xt_in[:, (n - 1) % XRING], xt_in[:, n % XRING], ALU.add).then_inc(acc_done, 2)
                elif c in POOL_CHUNKS and c > 1:
                    pool.wait_ge(xin[n % XRING], 16 * (n // XRING + 1))
                    pool.wait_ge(acc_done, NC * b + (2 if c == 3 else c if c != 6 else 5))
                    nc.gpsimd.tensor_tensor(acc(b), acc(b), xt_in[:, n % XRING], ALU.add).then_inc(acc_done, 2 if c - 1 in DVE_CHUNKS else 1)

            def split_hi(p):
                pool.wait_ge(xst[p % 2], 16 * (p // 2 + 1))
                if p >= XSR:
                    pool.wait_ge(xp_mm, KT * (p - XSR + 1))
                nc.gpsimd.tensor_scalar(xs[:, p % XSR, 0], xstage[:, p % 2], 1.0, 1.0, ALU.mult, ALU.mult).then_inc(xs_hi, 1)

            def split_lo(p):
                pool.wait_ge(xs_hi, p + 1)
                pool.wait_ge(xs_lo, p)
                nc.gpsimd.tensor_tensor(xs[:, p % XSR, 1], xstage[:, p % 2], xs[:, p % XSR, 0], ALU.subtract).then_inc(xs_lo, 1)

            def theta_hi(p):
                pool.wait_ge(th_sum, p + 1)
                pool.wait_ge(tp_saved, 64 * p)
                nc.gpsimd.tensor_scalar(tph[0:D], tp[0:D], 1.0, 1.0, ALU.mult, ALU.mult).then_inc(th_hi, 1)

            def theta_lo(p):
                pool.wait_ge(th_hi, p + 1)
                nc.gpsimd.tensor_tensor(tpl[0:D], tp[0:D], tph[0:D], ALU.subtract).then_inc(th_lo, 1)

            def bias_g(p):
                pool.wait_ge(g_raw, p + 1)
                if p >= GPRING:
                    pool.wait_ge(gt_mm, p - GPRING + 1)
                b = p // NC
                nc.gpsimd.tensor_scalar(gpool[:, p % GPRING], graw[:], smc(S_BG + b), 0.0, ALU.add, ALU.add).then_inc(g_bias, 1)

            def probs_hi(s):
                pool.wait_ge(ex2, s + 1)
                if s >= 2:
                    pool.wait_ge(pv_mm, s - 1)
                if s == 0:
                    pool.wait_ge(w_saved, 16)
                nc.gpsimd.tensor_scalar(pT[:, s % 2, 0], expT[:, s % 2], 1.0, 1.0, ALU.mult, ALU.mult).then_inc(pt_hi, 1)

            for p in range(LEAD):
                theta_lo(p)
                bias_g(p)
            split_hi(LEAD)
            split_lo(LEAD)
            for s in range(NS):
                t, q = divmod(s, TL)
                p = t + LEAD
                probs_hi(s)
                if q == 0 and 1 <= t and p - 1 < NP:
                    theta_hi(p - 1)
                    theta_lo(p - 1)
                if q == 1 and 1 <= t and p - 1 < NP:
                    bias_g(p - 1)
                if q == 2 and p + 1 < NP:
                    split_hi(p + 1)
                if q == 3 and p + 1 < NP:
                    split_lo(p + 1)

        @block.scalar
        def _(act):
            def gram_out(b):
                act.wait_ge(gram_mm, NC * (b + 1))
                if b >= 2:
                    act.wait_ge(mid_ev, STAGES * (b - 2) + 1)
                for m in range(KT):
                    ins = nc.scalar.activation(kk(hl_s(b))[:, m], psum[:, 4 + 2 * (b % 2) + m, 256:512], ACT.Copy, scale=1.0 / HW)
                ins.then_inc(gram_hl, 1)

            for n in range(NP):
                act.wait_ge(xin[n % XRING], 16 * (n // XRING + 1))
                if n >= XTR:
                    act.wait_ge(gram_mm, n - XTR + 1)
                nc.scalar.copy(xT(n)[:, :, 0], xt_in[:, n % XRING]).then_inc(tr_hi, 1)
                if n % NC == 0 and n > 0:
                    gram_out(n // NC - 1)
            gram_out(B - 1)

            def split_hi(p):
                act.wait_ge(xst[p % 2], 16 * (p // 2 + 1))
                if p < 2:
                    act.wait_ge(gram_mm, NP)
                if p == 6:
                    act.wait_ge(w_lo, B)
                    act.wait_ge(wo_done, 1)
                nc.scalar.copy(xs[:, p % XSR, 0], xstage[:, p % 2]).then_inc(xs_hi, 1)

            def theta_hi(p):
                act.wait_ge(th_sum, p + 1)
                if p >= 1:
                    act.wait_ge(tp_saved, 64 * p)
                nc.scalar.copy(tph[0:D], tp[0:D]).then_inc(th_hi, 1)

            def y_out(t, m):
                b = t // NC
                act.wait_ge(y_mm, KT * t + m + 1)
                if m == 0 and t >= 1:
                    act.wait_ge(stored, 16 * t)
                nc.scalar.activation(ostage[:, m], psum[:, B_Y + m], ACT.Identity,
                                     bias=smc(S_FB + 2 * b + m)).then_inc(y_ev, 1)

            def theta_out(p):
                b = p // NC
                act.wait_ge(th_mm, p + 1)
                if p >= 1:
                    act.wait_ge(th_lo, p)
                    act.wait_ge(phi_pool, p)
                else:
                    act.wait_ge(bias_ev, 1)
                nc.scalar.activation(tp[:], psum[0:2 * D, theta_bank(p)], ACT.Identity,
                                     bias=smc(S_BT + b, 1, 2 * D)).then_inc(th_half, 1)

            def weight_hi(b):
                act.wait_ge(w_sum, b + 1)
                nc.scalar.copy(kk(wmid(b, W_TA, KT * P))[:, :, 0:2 * D], kk(t32(b))[:, :, XG:EW])
                nc.scalar.copy(kk(wmid(b, W_GH, KT * DV)), kk(t32(b))[:, :, C:XG])
                nc.scalar.copy(kk(wmid(b, W_XH, KT * C)), kk(t32(b))[:, :, 0:C]).then_inc(w_hi, 1)

            def exponent1(e):
                m, r = divmod(e, TL)
                act.wait_ge(mx, e + 1)
                if r == 0 and m >= 2:
                    act.wait_ge(ln_done, m - 1)
                nc.scalar.activation(energy_banks(e), energy_banks(e), ACT.Exp, bias=nmax[:, m % 2, r:r + 1],
                                     accum_out=den[:, m % 2, r:r + 1]).then_inc(ex1, 1)
                if r == TL - 1:
                    act.wait_ge(ex1, e + 1)
                    if m >= 1:
                        act.wait_ge(sh_all, m)
                    nc.scalar.activation(lnden[:], den[:, m % 2], ACT.Ln).then_inc(ln_done, 1)

            def exponent2(s):
                act.wait_ge(e2_mm, s + 1)
                if s >= 2:
                    act.wait_ge(pt_lo, s - 1)
                nc.scalar.activation(expT[:, s % 2], psum[:, B_E2:B_E2 + 2], ACT.Exp).then_inc(ex2, 1)

            def attn_hi(t):
                act.wait_ge(pv_mm, TL * (t + 1))
                if t >= 1:
                    act.wait_ge(y_mm, KT * t)
                nc.scalar.copy(oh[:], psum[:, B_O]).then_inc(o_hi, 1)

            act.wait_ge(variance, 1)
            nc.scalar.activation(smc(S_RT, 2), smc(S_VAR, 2), ACT.Sqrt).then_inc(root, 1)
            nc.scalar.add_instruction(mybir.InstLoadActFuncSet(name=nc.get_next_instruction_name(), act_func_set_id=EXP_LN_SET))
            split_hi(0)
            weight_hi(0)
            split_hi(1)
            for p in range(LEAD):
                theta_out(p)
                theta_hi(p)
                if p + 2 < LEAD:
                    split_hi(p + 2)
                if 1 <= p < B:
                    weight_hi(p)
            for e in range(AHEAD - 1):
                exponent1(e)
            for s in range(NS + LAG + 4):
                t, q = divmod(s, TL)
                p = t + LEAD
                if s < NS:
                    exponent2(s)
                if s + AHEAD - 1 < NS:
                    exponent1(s + AHEAD - 1)
                if q == 0 and 2 <= t <= NP + 1:
                    y_out(t - 2, 1)
                if q == 1 and 1 <= t <= NP:
                    attn_hi(t - 1)
                if q == 2 and p < NP:
                    theta_out(p)
                if q == 3 and 1 <= t <= NP:
                    y_out(t - 1, 0)

        @block.tensor
        def _(pe):
            def split_product(o, wh, wl, vh, vl, start, stop):
                nc.tensor.matmul(o, wh, vh, start=start, stop=False)
                nc.tensor.matmul(o, wl, vh, start=False, stop=False)
                return nc.tensor.matmul(o, wh, vl, start=False, stop=stop)

            def gram(n):
                b, c = divmod(n, NC)
                pe.wait_ge(tr_lo, n + 1)
                if c == 0 and b >= 2:
                    pe.wait_ge(gram_ev, b - 1)
                for t in range(TL):
                    for m in range(KT):
                        ins = nc.tensor.matmul(psum[:, 4 + 2 * (b % 2) + m], xT(n)[:, t, 0, m * P:(m + 1) * P],
                                               xT(n)[:, t], start=(c == 0 and t == 0), stop=(c == NC - 1 and t == TL - 1))
                ins.then_inc(gram_mm, 1)

            def image_product(b, stage):
                i = STAGES * b + stage
                o, o2 = psum[:, 2 * (i % 2)], psum[:, 2 * (i % 2) + 1]
                if i == 0:
                    pe.wait_ge(consts, 16 * N_CONST)
                    pe.wait_ge(ones_set, 1)
                else:
                    pe.wait_ge(mid_ev, i)
                if stage == 0:
                    pe.wait_ge(tsum, b + 1)
                    pe.wait_ge(gram_ev, b + 1)
                    for k in range(KT):
                        nc.tensor.matmul(o[:, k:k + 1], tsum_s[:, k * P:(k + 1) * P], smc(S_ONE), start=True, stop=True)
                    hl = kk(hl_s(b))
                    for m in range(KT):
                        for k in range(KT):
                            ins = nc.tensor.transpose(o2[:, m * C + k * P:m * C + (k + 1) * P], hl[:, k, m * P:(m + 1) * P], ident[:])
                elif stage == 1:
                    for m in range(KT):
                        for k in range(KT):
                            nc.tensor.matmul(o[:, m * P:(m + 1) * P], e_s[:, k, m * P:(m + 1) * P], wpg_s[:, k, P:2 * P],
                                             start=(k == 0), stop=(k == KT - 1))
                    for k in range(KT):
                        nc.tensor.matmul(o[:, C:C + P], mrep_s[:, k], wpg_s[:, k, P:2 * P], start=(k == 0), stop=(k == KT - 1))
                    for k in range(KT):
                        ins = nc.tensor.matmul(o2[:, 0:1], wtT_s[:, k], smc(S_M + 2 * b + k), start=(k == 0), stop=(k == KT - 1))
                elif stage == 2:
                    for k in range(KT):
                        ins = nc.tensor.matmul(o[:, 0:P], wpg_s[:, k, 0:P], t1_s[:, k], start=(k == 0), stop=(k == KT - 1))
                elif stage == 3:
                    for m in range(KT):
                        nc.tensor.matmul(o[:, m * P:(m + 1) * P], wt_s[:, m * P:(m + 1) * P], mn_s, start=True, stop=True)
                    nc.tensor.matmul(o2[:, 0:C], mn_s, wt_s, start=True, stop=True)
                    ins = nc.tensor.matmul(o2[:, C:C + 2], mn_s, smc(S_TB + 2 * b, 2), start=True, stop=True)
                elif stage == 4:
                    for m in range(KT):
                        for k in range(KT):
                            nc.tensor.matmul(o[:, m * P:(m + 1) * P], e_s[:, k, m * P:(m + 1) * P], vt_s[:, k],
                                             start=(k == 0), stop=(k == KT - 1))
                    for m in range(KT):
                        ins = nc.tensor.matmul(o2[:, 2 * m:2 * m + 2], wwT_s[:, m * P:(m + 1) * P], v_s(b)[:, C:C + 2], start=True, stop=True)
                elif stage == 5:
                    for k in range(KT):
                        ins = nc.tensor.matmul(o[:, 0:P], vt_s[:, k], evt_s[:, k], start=(k == 0), stop=(k == KT - 1))
                else:
                    for m in range(KT):
                        ins = nc.tensor.matmul(o[:, m * P:(m + 1) * P], wwT_s[:, m * P:(m + 1) * P], f_s, start=True, stop=True)
                ins.then_inc(mid_mm, 1)

            for n in range(NP):
                gram(n)
                b, c = divmod(n, NC)
                if b >= 1 and c >= 1:
                    image_product(b - 1, c - 1)
            for stage in range(STAGES):
                image_product(B - 1, stage)

            pe.wait_ge(sw_ready, 1)
            for m in range(KT):
                nc.tensor.transpose(psum[:, B_E1, m * P:(m + 1) * P], sw_s[:, m], ident[:])
            for m in range(KT):
                ins = nc.tensor.matmul(psum[:, B_E1, C:EW], sw_s[:, m], ew_s[:, m, C:EW], start=(m == 0), stop=(m == KT - 1))
            ins.then_inc(su_mm, 1)

            def bias_product():
                d_v = smc(S_D, 2 * B).rearrange("p (b m) -> p b m", m=2)
                for m in range(KT):
                    nc.tensor.matmul(psum[0:2 * D, B_Y, 0:B], ew_s[:, m, XG:EW], d_v[:, :, m], start=(m == 0), stop=(m == KT - 1))
                for m in range(KT):
                    ins = nc.tensor.matmul(psum[:, B_Y, B:2 * B], ew_s[:, m, C:XG], d_v[:, :, m], start=(m == 0), stop=(m == KT - 1))
                ins.then_inc(bias_mm, 1)

            def weight_product(b):
                if b == 0:
                    pe.wait_ge(su_ev, 1)
                else:
                    pe.wait_ge(w_sum, b)
                for m in range(KT):
                    ins = nc.tensor.matmul(psum[:, B_E1 + m, 0:EW], v_s(b)[:, m * P:(m + 1) * P], su_s, start=True, stop=True)
                ins.then_inc(w_mm, 1)

            def project_theta(p, shifts=0):
                b = p // NC
                pe.wait_ge(xs_lo, p + 1)
                if p % NC == 0:
                    if b < 2:
                        pe.wait_ge(w_lo, b + 1)
                    else:
                        pe.wait_ge(wp_back, 16 * (b - 1))
                if p >= LEAD:
                    pe.wait_ge(sh_ev, shifts)
                elif p >= 2:
                    pe.wait_ge(th_sum, p - 1)
                o, w, x = psum[:, theta_bank(p)], wset[:, b % 2], xs[:, p % XSR]
                for k in range(KT):
                    nc.tensor.matmul(o, w[:, W_TA + k * P:W_TA + (k + 1) * P], x[:, 0, k], start=(k == 0), stop=False)
                    ins = nc.tensor.matmul(o, w[:, W_TB + k * P:W_TB + (k + 1) * P], x[:, 1, k], start=False, stop=(k == KT - 1))
                ins.then_inc(th_mm, 1)

            def project_g(p):
                b = p // NC
                if p >= LEAD:
                    pe.wait_ge(th_sum, p + 1)
                elif p >= 1:
                    pe.wait_ge(g_raw, p)
                else:
                    pe.wait_ge(bias_ev, 1)
                o, w, x = psum[:, g_bank(p)], wset[:, b % 2], xs[:, p % XSR]
                for k in range(KT):
                    ins = split_product(o, w[:, W_GH + k * DV:W_GH + (k + 1) * DV], w[:, W_GL + k * DV:W_GL + (k + 1) * DV],
                                        x[:, 0, k], x[:, 1, k], k == 0, k == KT - 1)
                ins.then_inc(g_mm, 1)

            def turn_g(p, gs, shifts):
                pe.wait_ge(g_bias, p + 1)
                if p >= 1:
                    pe.wait_ge(gt_lo, p)
                if gs > 0:
                    pe.wait_ge(g_raw, gs)
                if shifts > 0:
                    pe.wait_ge(sh_ev, shifts)
                nc.tensor.transpose(turned_g(p), gpool[:, p % GPRING], ident[:]).then_inc(gt_mm, 1)

            def turn_shift(m, turned, gs):
                pe.wait_ge(sh_two, m + 1)
                pe.wait_ge(gt_lo, turned)
                if gs > 0:
                    pe.wait_ge(g_raw, gs)
                if m >= 1:
                    pe.wait_ge(sh_ev, m)
                nc.tensor.transpose(turned_shift(m), shift2[:].rearrange("p h r -> p (h r)"), ident[:]).then_inc(sh_mm, 1)

            def energies1(e):
                m, r = divmod(e, TL)
                b = m // NC
                if r == 0:
                    pe.wait_ge(th4[m % TH4], 32 * (m // TH4 + 1))
                    if m % NC == 0:
                        pe.wait_ge(ph4, 48 * (b + 1))
                if e >= AHEAD - 1:
                    pe.wait_ge(ex1, e)
                elif e >= 2:
                    pe.wait_ge(ex1, e - 1)
                else:
                    pe.wait_ge(w_sum, B)
                for h in range(2):
                    ins = nc.tensor.matmul(energy_banks(e)[:, h], theta4[0:3 * D, m % TH4, r * P:(r + 1) * P],
                                           phi4[0:3 * D, b % 2, h * CH:(h + 1) * CH], start=True, stop=True)
                ins.then_inc(e1_mm, 1)

            def energies2(s):
                t, q = divmod(s, TL)
                b = t // NC
                if q == 0:
                    pe.wait_ge(sh_row[t % TH4], 16 * (t // TH4 + 1))
                if s >= 1:
                    pe.wait_ge(ex2, s)
                else:
                    pe.wait_ge(one_rows, 1)
                    pe.wait_ge(ex1, AHEAD - 2)
                    pe.wait_ge(th_sum, LEAD)
                    pe.wait_ge(g_raw, LEAD)
                for jj in range(2):
                    ins = nc.tensor.matmul(psum[:, B_E2 + jj], phi4[0:3 * D + 2, b % 2, (2 * q + jj) * P:(2 * q + jj + 1) * P],
                                           theta4[0:3 * D + 2, t % TH4], start=True, stop=True)
                ins.then_inc(e2_mm, 1)

            def attend(s):
                t, q = divmod(s, TL)
                b = t // NC
                pe.wait_ge(pt_lo, s + 1)
                if q == 0:
                    if t >= 1:
                        pe.wait_ge(o_lo, t)
                    if t % NC == 0:
                        pe.wait_ge(gt_lo, NC * (b + 1))
                for jj in range(2):
                    ins = split_product(psum[:, B_O], gT[:, b % 2, 0, 2 * q + jj], gT[:, b % 2, 1, 2 * q + jj],
                                        pT[:, s % 2, 0, jj], pT[:, s % 2, 1, jj],
                                        q == 0 and jj == 0, q == TL - 1 and jj == 1)
                ins.then_inc(pv_mm, 1)

            def x1_part(t, m):
                b = t // NC
                if t % NC == 0 and m == 0:
                    if b < 2:
                        pe.wait_ge(w_lo, b + 1)
                    else:
                        pe.wait_ge(wx_back, 16 * (b - 1))
                if t >= 1:
                    pe.wait_ge(y_ev, KT * (t - 1) + m + 1)
                w, x = wset[:, b % 2], xs[:, t % XSR]
                for k in range(KT):
                    cols = slice(k * C + m * P, k * C + (m + 1) * P)
                    ins = split_product(psum[:, B_Y + m], w[:, W_XH:W_XL][:, cols], w[:, W_XL:W_GH][:, cols],
                                        x[:, 0, k], x[:, 1, k], k == 0, False)
                ins.then_inc(xp_mm, 1)

            def convolve(t, m):
                pe.wait_ge(o_lo, t + 1)
                if t == 0 and m == 0:
                    pe.wait_ge(wo_done, 1)
                split_product(psum[:, B_Y + m], woh[:, m * P:(m + 1) * P], wol[:, m * P:(m + 1) * P], oh[:], ol[:],
                              False, True).then_inc(y_mm, 1)

            weight_product(0)
            bias_product()
            for p in range(LEAD):
                project_theta(p)
                project_g(p)
                if 1 <= p <= NC:
                    turn_g(p - 1, 0, 0)
                if 1 <= p < B:
                    weight_product(p)
            for e in range(AHEAD):
                energies1(e)
                if e == TL + 2:
                    turn_shift(0, NC, 0)
            for s in range(NS + LAG + 3):
                t, q = divmod(s, TL)
                p = t + LEAD
                if s < NS:
                    energies2(s)
                if q in (0, 1) and 1 <= t <= NP:
                    x1_part(t - 1, q)
                if q == 2 and p < NP:
                    project_theta(p, t + 2)
                if q == 3 and 1 <= t <= NP:
                    convolve(t - 1, 1)
                if LAG <= s < NS + LAG:
                    attend(s - LAG)
                if q == 0 and 1 <= t and t + NC - 1 < NP:
                    turn_g(t + NC - 1, min(p, NP), t + 1)
                if q == 1 and t + 1 < NP:
                    turn_shift(t + 1, min(t + NC, NP), min(p, NP))
                if q == 2 and 1 <= t <= NP:
                    convolve(t - 1, 0)
                if q == 3 and p < NP:
                    project_g(p)
                if s + AHEAD < NS:
                    energies1(s + AHEAD)

        @block.vector
        def _(dve):
            tt, ts, stt, cp = nc.vector.tensor_tensor, nc.vector.tensor_scalar, nc.vector.scalar_tensor_tensor, nc.vector.tensor_copy
            steps = [0]

            def then(ins):
                steps[0] += 1
                ins.then_inc(chain, 1)
                dve.wait_ge(chain, steps[0])

            def gram_sum(b):
                dve.wait_ge(gram_hl, b + 1)
                for m in range(KT):
                    ins = stt(kk(s1_s(b))[:, m], psum[:, 4 + 2 * (b % 2) + m, 0:256], 1.0 / HW, kk(hl_s(b))[:, m], ALU.mult, ALU.add)
                ins.then_inc(gram_ev, 1)

            def pixel_sum(b):
                dve.wait_ge(acc_done, NC * (b + 1))
                then(tt(acc(b), acc(b), dacc_s, ALU.add))
                if b >= 1:
                    dve.wait_ge(mid_mm, STAGES * (b - 1) + 1)
                nc.vector.tensor_reduce(tsum_s, acc(b).rearrange("p t c -> p c t"), AX.X, ALU.add).then_inc(tsum, 1)

            def image_result(b, stage):
                i = STAGES * b + stage
                o, o2 = psum[:, 2 * (i % 2)], psum[:, 2 * (i % 2) + 1]
                dve.wait_ge(mid_mm, i + 1)
                if i == 0:
                    dve.wait_ge(consts, 16 * N_CONST)
                if stage == 0:
                    then(cp(smc(S_M + 2 * b, 2), o[:, 0:2]))
                    for k in range(KT):
                        ts(mrep_s[:, k], ident[:], 0.0, smc(S_M + 2 * b + k), ALU.mult, ALU.add)
                    ins = tt(mid(O_E, 512), o2, s1_s(b), ALU.add)
                elif stage == 1:
                    for m in range(KT):
                        stt(t1_s[:, m], bgB_s, smc(S_M + 2 * b + m), o[:, m * P:(m + 1) * P], ALU.mult, ALU.add)
                    tt(gb_s, o[:, C:C + P], bgB_s, ALU.add)
                    cp(smc(S_TB + 2 * b), vc[:, V_BT:V_BT + 1])
                    ins = tt(smc(S_TB + 2 * b + 1), o2[:, 0:1], vc[:, V_BT:V_BT + 1], ALU.add)
                elif stage == 2:
                    ins = stt(mn_s, gb_s, vc[:, V_BP:V_BP + 1], o[:, 0:P], ALU.mult, ALU.add)
                elif stage == 3:
                    cp(mid(O_VT, 256), o[:, 0:C])
                    ins = cp(v_s(b), o2[:, 0:C + 2])
                elif stage == 4:
                    cp(mid(O_EVT, 256), o[:, 0:C])
                    ins = cp(smc(S_CW + 4 * b, 4), o2[:, 0:4])
                elif stage == 5:
                    ins = cp(f_s, o[:, 0:P])
                else:
                    for m in range(KT):
                        ins = nc.vector.tensor_tensor_reduce(out=ef[:, O_JUNK + m * P:O_JUNK + (m + 1) * P], in0=o[:, m * P:(m + 1) * P],
                                                             in1=ww_s[:, m], scale=1.0, scalar=0.0, op0=ALU.mult, op1=ALU.add,
                                                             accum_out=smc(S_Q + 2 * b + m))
                ins.then_inc(mid_ev, 1)

            for n in range(NP):
                b, c = divmod(n, NC)
                dve.wait_ge(tr_hi, n + 1)
                tt(xT(n)[:, :, 1], xt_in[:, n % XRING], xT(n)[:, :, 0], ALU.subtract).then_inc(tr_lo, 1)
                if b >= 1 and c == 0:
                    if b >= 2:
                        image_result(b - 2, STAGES - 1)
                    gram_sum(b - 1)
                    pixel_sum(b - 1)
                if b >= 1 and c >= 2:
                    image_result(b - 1, c - 2)
                if c == DVE_CHUNKS[1]:
                    m = n - DVE_CHUNKS[1] + DVE_CHUNKS[0]
                    tt(dacc_s, xt_in[:, m % XRING], xt_in[:, n % XRING], ALU.add).then_inc(dacc, 1)
            image_result(B - 2, STAGES - 1)
            gram_sum(B - 1)
            pixel_sum(B - 1)
            for stage in range(STAGES):
                image_result(B - 1, stage)

            def per_image(off, m):
                return sm[:, off:off + 2 * B].rearrange("p (b m) -> p b m", m=2)[:, :, m]

            def all_images(off):
                return smc(off, 2 * B).rearrange("p (b m) -> p b m", m=2)

            cw = smc(S_CW, 4 * B).rearrange("p (b m j) -> p b m j", m=2, j=2)
            dve.wait_ge(mid_ev, STAGES * B)
            tt(all_images(S_AM), cw[:, :, :, 1], cw[:, :, :, 0], ALU.subtract)
            for m in range(KT):
                ts(per_image(S_WB, m), cw[:, :, m, 1], vc[:, V_WB + m:V_WB + m + 1], None, ALU.add)
                ins = ts(per_image(S_CB, m), cw[:, :, m, 0], vc[:, V_WB + m:V_WB + m + 1], None, ALU.add)
            then(ins)
            nc.vector.tensor_reduce(smc(S_MU, 2), smc(S_WB, 8).rearrange("p (b m) -> p m b", m=2), AX.X, ALU.add)
            then(tt(smc(S_AM, 8), smc(S_AM, 8), smc(S_AM, 8), ALU.mult))
            ts(smc(S_MU, 2), smc(S_MU, 2), 1.0 / B, None, ALU.mult)
            then(tt(smc(S_Q, 8), smc(S_Q, 8), smc(S_AM, 8), ALU.subtract))
            for m in range(KT):
                ins = ts(per_image(S_DEV, m), per_image(S_WB, m), smc(S_MU + m), None, ALU.subtract)
            then(ins)
            then(tt(smc(S_DEV, 8), smc(S_DEV, 8), smc(S_DEV, 8), ALU.mult))
            then(tt(smc(S_DEV, 8), smc(S_DEV, 8), smc(S_Q, 8), ALU.add))
            then(nc.vector.tensor_reduce(smc(S_VAR, 2), smc(S_DEV, 8).rearrange("p (b m) -> p m b", m=2), AX.X, ALU.add))
            ts(smc(S_VAR, 2), smc(S_VAR, 2), 1.0 / B, BN_EPS, ALU.mult, ALU.add).then_inc(variance, 1)
            dve.wait_ge(root, 1)
            v, r, h = smc(S_VAR, 2), smc(S_S, 2), smc(S_DEV, 2)
            then(nc.vector.reciprocal(r, smc(S_RT, 2)))
            then(tt(h, r, r, ALU.mult))
            then(tt(h, h, v, ALU.mult))
            then(ts(h, h, -0.5, 1.5, ALU.mult, ALU.add))
            then(tt(r, r, h, ALU.mult))
            then(tt(r, r, vc[:, V_GAM:V_GAM + 2], ALU.mult))
            for m in range(KT):
                ts(sw_s[:, m], ww_s[:, m], smc(S_S + m), None, ALU.mult)
            for m in range(KT):
                ins = ts(per_image(S_D, m), per_image(S_CB, m), smc(S_MU + m), smc(S_S + m), ALU.subtract, ALU.mult)
            then(ins)
            for m in range(KT):
                ins = ts(per_image(S_D, m), per_image(S_D, m), vc[:, V_BETA + m:V_BETA + m + 1], None, ALU.add)
            ins.then_inc(sw_ready, 1)
            dve.wait_ge(sw_ready, 1)
            then(ts(smc(S_GB, 2), vc[:, V_BO:V_BO + 2], vc[:, V_G:V_G + 1], None, ALU.mult))
            for m in range(KT):
                ts(per_image(S_FB, m), per_image(S_D, m), smc(S_GB + m), None, ALU.add)
            dve.wait_ge(su_mm, 1)
            cp(su_s, psum[:, B_E1, 0:EW]).then_inc(su_ev, 1)

            def weight_sum(b):
                dve.wait_ge(w_mm, b + 1)
                tt(t32(b).rearrange("p (k n) -> p k n", k=KT), psum[:, B_E1:B_E1 + 2, 0:EW], ew_s, ALU.add).then_inc(w_sum, 1)

            def weight_lo(b):
                dve.wait_ge(w_hi, b + 1)
                ta, tb = kk(wmid(b, W_TA, KT * P)), kk(wmid(b, W_TB, KT * P))
                ts(tb[:, :, 0:2 * D], kk(ident[:]), 0.0, None, ALU.mult)
                cp(tb[:, :, 2 * D:4 * D], kk(t32(b))[:, :, XG:EW])
                tt(ta[:, :, 2 * D:4 * D], kk(t32(b))[:, :, XG:EW], ta[:, :, 0:2 * D], ALU.subtract)
                tt(kk(wmid(b, W_GL, KT * DV)), kk(t32(b))[:, :, C:XG], kk(wmid(b, W_GH, KT * DV)), ALU.subtract)
                tt(kk(wmid(b, W_XL, KT * C)), kk(t32(b))[:, :, 0:C], kk(wmid(b, W_XH, KT * C)), ALU.subtract).then_inc(w_lo, 1)

            def split_x(p):
                dve.wait_ge(xs_hi, p + 1)
                tt(xs[:, p % XSR, 1], xstage[:, p % 2], xs[:, p % XSR, 0], ALU.subtract).then_inc(xs_lo, 1)

            weight_sum(0)
            weight_lo(0)
            split_x(0)
            dve.wait_ge(bias_mm, 1)
            ts(smc(S_BT, B, 2 * D), psum[0:2 * D, B_Y, 0:B], vc[0:2 * D, V_BTP:V_BTP + 1], None, ALU.add)
            ts(smc(S_BG, B), psum[:, B_Y, B:2 * B], vc[:, V_BG:V_BG + 1], None, ALU.add).then_inc(bias_ev, 1)
            then(ts(mid(O_GWO, C), wo_s, vc[:, V_G:V_G + 1], None, ALU.mult))
            then(cp(woh[:], mid(O_GWO, C)))
            tt(wol[:], mid(O_GWO, C), woh[:], ALU.subtract).then_inc(wo_done, 1)

            def theta_sum(p):
                dve.wait_ge(th_half, p + 1)
                tt(tp[:], psum[2 * D:4 * D, theta_bank(p)], tp[:], ALU.add).then_inc(th_sum, 1)

            def phi_out(p):
                dve.wait_ge(th_sum, p + 1)
                if p >= 1:
                    dve.wait_ge(tp_saved, 64 * p)
                nc.vector.tensor_reduce(phip[D:2 * D].rearrange("p (r c) -> p r c", c=W_IMG // 2),
                                        tp[D:2 * D].rearrange("p (r i c j) -> p r c i j", i=2, j=2, c=W_IMG // 2),
                                        AX.XY, ALU.max).then_inc(phi_pool, 1)
                dve.wait_ge(phi_pool, p + 1)
                cp(phh[D:2 * D], phip[D:2 * D]).then_inc(phi_hi, 1)
                dve.wait_ge(phi_hi, p + 1)
                tt(phl[D:2 * D], phip[D:2 * D], phh[D:2 * D], ALU.subtract).then_inc(phi_lo, 1)

            def pool_g(p):
                dve.wait_ge(g_mm, p + 1)
                if p >= 1:
                    dve.wait_ge(g_bias, p)
                nc.vector.tensor_reduce(graw[:].rearrange("p (r c) -> p r c", c=W_IMG // 2),
                                        psum[:, g_bank(p)].rearrange("p (r i c j) -> p r c i j", i=2, j=2, c=W_IMG // 2),
                                        AX.XY, ALU.max).then_inc(g_raw, 1)

            def split_g(p):
                b, c = divmod(p, NC)
                dve.wait_ge(gt_mm, p + 1)
                if b >= 2:
                    dve.wait_ge(pv_mm, TL * NC * (b - 1))
                cp(gT[:, b % 2, 0, c], turned_g(p)).then_inc(gt_hi, 1)
                dve.wait_ge(gt_hi, p + 1)
                tt(gT[:, b % 2, 1, c], turned_g(p), gT[:, b % 2, 0, c], ALU.subtract).then_inc(gt_lo, 1)

            def row_max(e):
                m, r = divmod(e, TL)
                dve.wait_ge(e1_mm, e + 1)
                if m >= 2 and r == 0:
                    dve.wait_ge(ex1, TL * (m - 1))
                    dve.wait_ge(sh_all, m - 1)
                nc.vector.tensor_reduce(nmax[:, m % 2, r:r + 1], energy_banks(e), AX.XY, ALU.max, negate=True).then_inc(mx, 1)

            def make_shift(m):
                dve.wait_ge(ln_done, m + 1)
                tt(shift[:], nmax[:, m % 2], lnden[:], ALU.subtract).then_inc(sh_all, 1)
                dve.wait_ge(sh_all, m + 1)
                cp(shift_r[:], shift[:]).then_inc(sh_hi, 1)
                dve.wait_ge(sh_hi, m + 1)
                if m >= 1:
                    dve.wait_ge(sh_mm, m)
                cp(shift2[:, 0], shift_r[:])
                tt(shift2[:, 1], shift[:], shift_r[:], ALU.subtract).then_inc(sh_two, 1)

            def shift_out(m):
                dve.wait_ge(sh_mm, m + 1)
                if m >= 1:
                    dve.wait_ge(sh_saved, 16 * m)
                cp(shiftT[:], turned_shift(m)).then_inc(sh_ev, 1)

            def probs_lo(s):
                dve.wait_ge(pt_hi, s + 1)
                tt(pT[:, s % 2, 1], expT[:, s % 2], pT[:, s % 2, 0], ALU.subtract).then_inc(pt_lo, 1)

            def attn_lo(t):
                dve.wait_ge(o_hi, t + 1)
                tt(ol[:], psum[:, B_O], oh[:], ALU.subtract).then_inc(o_lo, 1)

            for p in range(LEAD):
                theta_sum(p)
                if p + 1 < LEAD:
                    split_x(p + 1)
                phi_out(p)
                pool_g(p)
                if 1 <= p < B:
                    weight_sum(p)
                if 1 <= p <= NC:
                    split_g(p - 1)
                if 1 <= p < B:
                    weight_lo(p)
            for e in range(AHEAD - 1):
                row_max(e)
                if e == TL + 1:
                    make_shift(0)
            shift_out(0)
            for s in range(NS + LAG + 2):
                t, q = divmod(s, TL)
                p = t + LEAD
                if s + AHEAD - 1 < NS:
                    row_max(s + AHEAD - 1)
                if q == 0 and 1 <= t and p - 1 < NP:
                    pool_g(p - 1)
                if q == 3 and p < NP:
                    theta_sum(p)
                if 1 <= s <= NS:
                    probs_lo(s - 1)
                if q == 0 and 1 <= t and t + NC - 1 < NP:
                    split_g(t + NC - 1)
                if q == 0 and t + 1 < NP:
                    make_shift(t + 1)
                if q == 1 and t + 1 < NP:
                    shift_out(t + 1)
                if q == 1 and 1 <= t <= NP:
                    attn_lo(t - 1)
                if q == 2 and 1 <= t and p - 1 < NP:
                    phi_out(p - 1)


def kernel(**inputs):
    import numpy as np
    import concourse.bacc as bacc
    from concourse.bass_utils import run_bass_kernel_spmd

    def a(name):
        return np.asarray(inputs[name])

    def tiles(w):
        return np.ascontiguousarray(w.reshape(KT, P, -1).transpose(1, 0, 2).reshape(P, -1))

    def col(v):
        return tiles(v.reshape(-1, 1)) if v.size == C else v.reshape(-1, 1)

    xin = a("x").reshape(B, C, HW)
    f = xin.dtype
    btp = np.zeros((P, 1), f)
    btp[0:D, 0] = a("L1_conv_theta_b")
    btp[D:2 * D, 0] = a("L1_conv_phi_b")
    w1T = np.concatenate([a("L1_conv_g_w"), a("L1_conv_theta_w"), a("L1_conv_phi_w")]).T
    arrays = {
        "xT": np.ascontiguousarray(xin.transpose(0, 2, 1)),
        "x": xin,
        "wpgT": tiles(np.concatenate([a("L0_conv_phi_w"), a("L0_conv_g_w")]).T),
        "wt": a("L0_conv_theta_w"),
        "wtT": tiles(a("L0_conv_theta_w").T),
        "wwT": np.ascontiguousarray(a("L0_conv_w_w").T),
        "ww": tiles(a("L0_conv_w_w")),
        "ew": tiles(np.concatenate([np.eye(C, dtype=f), w1T], 1)),
        "woT": np.ascontiguousarray(a("L1_conv_out_w").T),
        "bgB": np.repeat(a("L0_conv_g_b").reshape(1, P), P, 0),
        "cols": np.ascontiguousarray(np.concatenate(
            [col(a("L0_conv_theta_b")), col(a("L0_conv_w_b")), col(a("L0_conv_gamma")), col(a("L0_conv_beta")),
             col(a("L1_conv_out_b")), btp, col(a("L1_conv_g_b")), np.repeat(a("L1_conv_gamma").reshape(1, 1), P, 0),
             col(a("L0_conv_phi_b"))], 1)),
        "eye": np.eye(P, dtype=f),
    }
    nc = bacc.Bacc("TRN2", target_bir_lowering=False, num_devices=1)
    args = [nc.dram_tensor("in_" + n, v.shape, mybir.dt.from_np(v.dtype), kind="ExternalInput").ap() for n, v in arrays.items()]
    out = nc.dram_tensor("out_y", (B, C, HW), F32, kind="ExternalOutput").ap()
    nonlocal_then_attention(nc, *args, out)
    r = run_bass_kernel_spmd(nc, [{"in_" + n: np.ascontiguousarray(v) for n, v in arrays.items()}], core_ids=[0])
    return r.results[0]["out_y"].reshape(B, C, 64, 64)
```

```python
from contextlib import ExitStack

import concourse.bass as bass
from concourse import mybir

F32 = mybir.dt.float32
F32R = mybir.dt.float32r
ALU = mybir.AluOpType
ACT = mybir.ActivationFunctionType
AX = mybir.AxisListType

P = 128
B, C, HW = 4, 256, 4096
W_IMG = 64
KT = C // P
CH = 512
NC = HW // CH
NP = B * NC
TL = CH // P
J = HW // 4
JC = J // P
D = C // 8
DV = C // 2
W1 = 2 * D + DV
PCH = CH // 4
NS = NP * TL
LEAD = 11
PRELOAD = 10
EARLY_SPLITS = 6
AHEAD = 2 * TL
EARLIEST = 2
LAG = 2
BN_EPS = 1e-5
EXP_LN_SET = 6

XRING = 8
XTR = 4
XSR = LEAD + 3
GPRING = 4
TH4 = 4
O_ACC, O_DACC, O_TSUM, O_S1, O_HL = 0, 2048, 3072, 3328, 4352
C2 = C + 4
O_E = O_HL + 1024
O_T1 = O_E + KT * C2
O_VT = O_T1 + C
O_VE = O_VT + C
O_A = O_VE + C2
O_GB = O_A + KT * C
O_Q = O_GB + P
O_R = O_Q + KT * C2
O_JUNK = O_R + C2
O_CST = O_JUNK + KT * C
O_WP = O_CST
O_WG = O_WP + C
O_WTB = O_WG + C
O_WWT = O_WTB + C2
O_WW = O_WWT + C
O_EW = O_WW + C
O_WO = O_EW + KT * (C + W1)
O_BGB = O_WO + C
O_T32 = O_BGB + P
O_GWO = O_T32 + 2 * KT * (C + W1)
O_END = O_GWO + C
O_V, O_SU, O_SW = 0, B * C2, B * C2 + C + W1
EW = C + W1
XG = C + DV
W_XH, W_XL = 0, KT * C
W_GH, W_GL = 2 * KT * C, 2 * KT * C + KT * DV
W_TA, W_TB = 2 * KT * XG, 2 * KT * XG + KT * P
W_SET = W_TB + KT * P
W_X = W_GH
S_M, S_Q, S_CW, S_U, S_MU, S_DEV, S_VAR, S_S, S_D, S_FB, S_BT, S_BG, S_GB, S_RT, S_AM, S_ONE, S_W = \
    0, 8, 16, 32, 40, 42, 50, 52, 54, 62, 70, 74, 78, 80, 82, 90, 91
V_WB, V_GAM, V_BETA, V_BO, V_BTP, V_BG, V_G, V_BP, V_W = 0, 2, 4, 6, 8, 9, 10, 11, 12
STAGES = 5


def nonlocal_then_attention(nc, xT_in, x, wp, wgT, wtb, wwT, ww, ew, woT, bgB, cols, eye, out):
    with ExitStack() as ctx:
        def sb(name, shape, dt=F32):
            return ctx.enter_context(nc.sbuf_tensor(name, shape, dt))

        def sem(name):
            return ctx.enter_context(nc.semaphore(name))

        with (nc.sbuf_tensor("in_ring", [P, XRING, TL, C], F32) as xt_in,
              nc.sbuf_tensor("xT_more", [P, 2 * 2 * TL * C], F32R) as xT_more,
              nc.sbuf_tensor("middle", [P, O_END], F32) as middle):
            pass
        with nc.sbuf_tensor("xl0", [P, XSR // 2, 2, KT, CH], F32) as xl0, nc.sbuf_tensor("xl1", [P, XSR // 2, 2, KT, CH], F32) as xl1:
            pass
        xs_halves = [sb(f"xs{i}", [P, XSR // 2, 2, KT, CH], F32R) for i in range(2)]

        def xs(p):
            i = p % XSR
            return xs_halves[i // (XSR // 2)][:, i % (XSR // 2)]

        def xl(p):
            i = p % XSR
            return (xl0, xl1)[i // (XSR // 2)][:, i % (XSR // 2), 1]

        ef = sb("ef", [P, 2 * 2 * CH])
        expT = ef[:, :].rearrange("p (a j n) -> p a j n", a=2, j=2)
        ptf = sb("ptf", [P, 2 * 2 * 2 * CH], F32R)
        xT_half = [m.rearrange("p (a t h c) -> p a t h c", a=2, t=TL, h=2)
                   for m in (ptf[:, :], xT_more[:, :])]
        pT = ptf[:, :].rearrange("p (a h j n) -> p a h j n", a=2, h=2, j=2)
        theta4 = sb("theta4", [P, TH4, CH], F32R)
        phi4 = sb("phi4", [P, 2, J], F32R)
        gpool = sb("gpool", [P, GPRING, PCH])
        graw = sb("graw", [P, PCH])
        gT = sb("gT", [P, 2, 2, JC, DV], F32R)
        tp = sb("tp", [2 * D, CH])
        phip = sb("phip", [2 * D, PCH])
        tph = sb("tph", [2 * D, CH], F32R)
        tpl = sb("tpl", [2 * D, CH], F32R)
        phh = sb("phh", [2 * D, PCH], F32R)
        phl = sb("phl", [2 * D, PCH], F32R)
        oh = sb("oh", [P, CH], F32R)
        ol = sb("ol", [P, CH], F32R)
        ostage = sb("ostage", [P, KT, CH])
        wset = sb("wset", [P, 2, W_SET], F32R)
        woh = sb("woh", [P, C], F32R)
        wol = sb("wol", [P, C], F32R)
        ident = sb("ident", [P, P])
        sm = sb("sm", [P, S_W])
        vc = sb("vc", [P, V_W])
        nmax = sb("nmax", [P, 2, TL])
        den = sb("den", [P, 2, TL])
        lnden = sb("lnden", [P, TL])
        shift = sb("shift", [P, TL])
        shift_r = sb("shift_r", [P, TL], F32R)
        shift2 = sb("shift2", [P, 2, TL])
        shiftT = sb("shiftT", [2 * TL, P])

        psum = ctx.enter_context(nc.psum_tensor("psum", [P, 8, 512], F32))
        B_E2, B_E1, B_O, B_TG, B_Y = 0, 2, 4, 5, 6
        EARLY_BANKS = (B_E1, B_E2, B_O, B_E1, B_E2, B_O, B_E1, B_O)

        scr_theta = nc.dram_tensor("scr_theta", [NP, 2 * D, CH], F32)
        scr_phi = nc.dram_tensor("scr_phi", [B, 2, D, J], F32)
        scr_shift = nc.dram_tensor("scr_shift", [NP, 2 * TL, P], F32)
        scr_w = nc.dram_tensor("scr_w", [2, P, W_SET], F32)

        xin = [sem(f"xin{i}") for i in range(XRING)]
        consts = sem("consts")
        tr_hi = sem("tr_hi")
        tr_lo = sem("tr_lo")
        acc_done = sem("acc_done")
        dacc = sem("dacc")
        tsum = sem("tsum")
        ones_set = sem("ones_set")
        q_mm = sem("q_mm")
        q_ev = sem("q_ev")
        gram_mm = sem("gram_mm")
        gram_hl = sem("gram_hl")
        gram_ev = sem("gram_ev")
        mid_mm = sem("mid_mm")
        mid_ev = sem("mid_ev")
        chain = sem("chain")
        variance = sem("variance")
        root = sem("root")
        sw_ready = sem("sw_ready")
        d_ready = sem("d_ready")
        su_mm = sem("su_mm")
        su_ev = sem("su_ev")
        bias_mm = sem("bias_mm")
        bias_ev = sem("bias_ev")
        w_mm = sem("w_mm")
        w_sum = sem("w_sum")
        w_hi = sem("w_hi")
        w_lo = sem("w_lo")
        w_saved = sem("w_saved")
        wx_back = sem("wx_back")
        wp_back = sem("wp_back")
        xst = [sem(f"xst{i}") for i in range(XSR)]
        xs_hi = sem("xs_hi")
        xs_lo = sem("xs_lo")
        xp_mm = sem("xp_mm")
        th_mm = sem("th_mm")
        th_half = sem("th_half")
        th_sum = sem("th_sum")
        phi_pool = sem("phi_pool")
        phi_hi = sem("phi_hi")
        phi_lo = sem("phi_lo")
        th_hi = sem("th_hi")
        th_lo = sem("th_lo")
        tp_saved = [sem(f"tp_saved{i}") for i in range(2)]
        g_mm = sem("g_mm")
        g_raw = sem("g_raw")
        g_bias = sem("g_bias")
        gt_mm = sem("gt_mm")
        gt_hi = sem("gt_hi")
        gt_lo = sem("gt_lo")
        wo_done = sem("wo_done")
        th4 = [sem(f"th4_{i}") for i in range(TH4)]
        ph4 = sem("ph4")
        one_rows = sem("one_rows")
        e1_mm = sem("e1_mm")
        mx = sem("mx")
        ex1 = sem("ex1")
        ln_done = sem("ln_done")
        sh_all = sem("sh_all")
        sh_hi = sem("sh_hi")
        sh_two = sem("sh_two")
        sh_mm = sem("sh_mm")
        sh_ev = sem("sh_ev")
        sh_saved = sem("sh_saved")
        sh_row = [sem(f"sh_row{i}") for i in range(TH4)]
        e2_mm = sem("e2_mm")
        ex2 = sem("ex2")
        pt_hi = sem("pt_hi")
        pt_lo = sem("pt_lo")
        pv_mm = sem("pv_mm")
        o_hi = sem("o_hi")
        o_lo = sem("o_lo")
        y_mm = sem("y_mm")
        y_ev = sem("y_ev")
        stored = sem("stored")

        x_v = x.rearrange("b (k p) n -> b p k n", p=P)
        xT_v = xT_in.rearrange("b (c p t) k -> b c p t k", c=NC, p=P)
        out_v = out.rearrange("b (k p) n -> b p k n", p=P)

        def mid(off, n):
            return middle[:, off:off + n]

        def kk(ap):
            return ap.rearrange("p (k n) -> p k n", k=KT)

        wgT_s, ww_s, ew_s = kk(mid(O_WG, C)), kk(mid(O_WW, C)), kk(mid(O_EW, KT * EW))
        wp_s, wtb_s, wwT_s, wo_s, bgB_s = mid(O_WP, C), mid(O_WTB, C + 1), mid(O_WWT, C), mid(O_WO, C), mid(O_BGB, P)
        e_s, q_s = kk(mid(O_E, KT * C2)), kk(mid(O_Q, KT * C2))
        t1_s, vt_s, a_s = kk(mid(O_T1, C)), kk(mid(O_VT, C)), kk(mid(O_A, KT * C))
        ve_s, gb_s, r_s, tsum_s = mid(O_VE, C + 2), middle[0:1, O_GB:O_GB + P], middle[0:1, O_R:O_R + C + 1], mid(O_TSUM, C)
        su_s, sw_s = ef[:, O_SU:O_SU + EW], kk(ef[:, O_SW:O_SW + C])

        def v_s(b):
            return ef[:, O_V + C2 * b:O_V + C2 * b + C + 1]

        def acc(b):
            return mid(O_ACC + 1024 * (b % 2), 1024).rearrange("p (t c) -> p t c", t=TL)

        dacc_s = mid(O_DACC, 1024).rearrange("p (t c) -> p t c", t=TL)

        def s1_s(b):
            return mid(O_S1 + 512 * (b % 2), 512)

        def hl_s(b):
            return mid(O_HL + 512 * (b % 2), 512)

        def t32(b):
            return mid(O_T32 + KT * EW * (b % 2), KT * EW)

        def xT(n):
            return xT_half[n % XTR // 2][:, n % 2]

        def smc(off, n=1, parts=P):
            return sm[0:parts, off:off + n]

        def wmid(b, off, n):
            if b < 2:
                return wset[:, b, off:off + n]
            return ptf[:, (b - 2) * W_SET + off:(b - 2) * W_SET + off + n]

        const_loads = ((ident[:], eye), (vc[:], cols), (mid(O_WP, C), wp), (wtb_s, wtb), (mid(O_WG, C), wgT), (mid(O_BGB, P), bgB),
                       (mid(O_WWT, C), wwT), (mid(O_WW, C), ww), (mid(O_EW, KT * EW), ew), (mid(O_WO, C), woT))
        N_CONST = len(const_loads)
        POOL_CHUNKS = (0, 1, 3, 4, 6, 7)
        DVE_CHUNKS = (2, 5)

        def parts(p):
            if p < LEAD and p % 2 == 1:
                return oh[0:D], ol[0:D], oh[D:2 * D, 0:PCH], ol[D:2 * D, 0:PCH]
            return tph[0:D], tpl[0:D], phh[D:2 * D], phl[D:2 * D]

        def wait_saved(engine, p):
            if p >= 0:
                engine.wait_ge(tp_saved[p % 2], 64 * (p // 2 + 1))

        def last_with_parts(p):
            return p - 2 if p < LEAD else p - 1

        def half_columns(half):
            return slice(C, EW) if half == 0 else slice(0, C)

        def half_banks(half):
            return B_E1 if half == 0 else B_E2

        def weights_beside(p):
            return [(0, 1)] if p == 0 else [(p, 0), (p, 1)] if p < B else []

        def high_beside(p):
            return [p + 3] if EARLY_SPLITS <= p + 3 < LEAD else []

        def low_beside(p):
            return [p + 2] if EARLY_SPLITS <= p + 2 < LEAD else []

        def theta_bank(p):
            return B_TG if p >= LEAD else B_O + p % 2

        def g_bank(p):
            return B_TG if p >= LEAD else B_Y

        def turned_g(p):
            return psum[:, B_TG if p >= NC else B_Y + 1, 0:P]

        def turned_shift(m):
            return psum[0:2 * TL, B_TG if m >= 1 else B_Y + 1, 0:P]

        def energy_banks(e):
            o = EARLY_BANKS[e] if e < AHEAD else B_E1
            return psum[:, o:o + 2]

        block = ctx.enter_context(nc.Block())

        @block.sync
        def _(sp):
            for n in range(NP):
                b, c = divmod(n, NC)
                if n >= XRING:
                    m = n - XRING
                    sp.wait_ge(tr_lo, m + 1)
                    if c in POOL_CHUNKS:
                        sp.wait_ge(acc_done, NC * (m // NC) + c + 1)
                    else:
                        sp.wait_ge(dacc, m // NC + 1)
                sp.dma_start(xt_in[:, n % XRING], xT_v[b, c]).then_inc(xin[n % XRING], 16)
                if n >= 2 and n - 2 < N_CONST:
                    sp.dma_start(*const_loads[n - 2]).then_inc(consts, 16)

            def load_x(p):
                b, c = divmod(p, NC)
                if p < NC // 2:
                    sp.wait_ge(tr_lo, NP - NC + 2 * (p + 1))
                    sp.wait_ge(dacc, B)
                    sp.wait_ge(acc_done, NP - NC + 2 * (p + 1))
                elif p == NC // 2:
                    sp.wait_ge(gram_mm, NP)
                elif p == EARLY_SPLITS:
                    sp.wait_ge(mid_ev, STAGES * B)
                elif p == PRELOAD:
                    sp.wait_ge(w_lo, 2 * B)
                    sp.wait_ge(wo_done, 1)
                elif p >= XSR:
                    sp.wait_ge(xp_mm, KT * (p - XSR + 1))
                sp.dma_start(xl(p), x_v[b, :, :, c * CH:(c + 1) * CH]).then_inc(xst[p % XSR], 16)

            def save_tp(p):
                b, c = divmod(p, NC)
                th_h, th_l, ph_h, ph_l = parts(p)
                sp.wait_ge(th_lo, p + 1)
                sp.dma_start(scr_theta[p, 0:D], th_h.bitcast(F32)).then_inc(tp_saved[p % 2], 16)
                sp.dma_start(scr_theta[p, D:2 * D], th_l.bitcast(F32)).then_inc(tp_saved[p % 2], 16)
                sp.wait_ge(phi_lo, p + 1)
                sp.dma_start(scr_phi[b, 0, :, c * PCH:(c + 1) * PCH], ph_h.bitcast(F32)).then_inc(tp_saved[p % 2], 16)
                sp.dma_start(scr_phi[b, 1, :, c * PCH:(c + 1) * PCH], ph_l.bitcast(F32)).then_inc(tp_saved[p % 2], 16)

            def load_theta(m):
                if m >= TH4:
                    sp.wait_ge(e2_mm, TL * (m - TH4 + 1))
                wait_saved(sp, m)
                sp.dma_start(theta4[0:2 * D, m % TH4].bitcast(F32), scr_theta[m]).then_inc(th4[m % TH4], 16)
                sp.dma_start(theta4[2 * D:3 * D, m % TH4].bitcast(F32), scr_theta[m, 0:D]).then_inc(th4[m % TH4], 16)

            def load_phi(b):
                wait_saved(sp, NC * (b + 1) - 2)
                wait_saved(sp, NC * (b + 1) - 1)
                if b >= 2:
                    sp.wait_ge(e2_mm, TL * NC * (b - 1))
                for q in range(3):
                    sp.dma_start(phi4[D * q:D * (q + 1), b % 2].bitcast(F32), scr_phi[b, q // 2]).then_inc(ph4, 16)

            def row_shift(m):
                sp.wait_ge(sh_ev, m + 1)
                sp.dma_start(scr_shift[m], shiftT[:]).then_inc(sh_saved, 16)
                sp.wait_ge(sh_saved, 16 * (m + 1))
                sp.dma_start(theta4[3 * D:3 * D + 2, m % TH4].bitcast(F32),
                             scr_shift[m].rearrange("(h r) n -> h (r n)", h=2)).then_inc(sh_row[m % TH4], 16)

            for p in range(PRELOAD):
                load_x(p)
            for p in range(LEAD):
                if p >= 1:
                    save_tp(p - 1)
                if p == B:
                    load_x(PRELOAD)
                if B < p <= NC:
                    a, half = divmod(p - B - 1, 2)
                    sp.dma_start(scr_w[a, :, half * W_X:(half + 1) * W_X],
                                 ptf[:, a * W_SET + half * W_X:a * W_SET + (half + 1) * W_X].bitcast(F32)).then_inc(w_saved, 16)
                if p == NC:
                    load_phi(0)
                    load_theta(0)
                if p == NC + 1:
                    load_theta(1)
                    load_theta(2)
                if p == LEAD - 1:
                    load_x(LEAD)
            save_tp(LEAD - 1)
            row_shift(0)
            load_x(LEAD + 1)
            for t in range(NP + 2):
                p = t + LEAD
                if t >= 2:
                    b, c = divmod(t - 2, NC)
                    sp.wait_ge(y_ev, KT * (t - 1))
                    sp.dma_start(out_v[b, :, :, c * CH:(c + 1) * CH], ostage[:]).then_inc(stored, 16)
                if t + 3 < NP:
                    load_theta(t + 3)
                for b in (2, 3):
                    if t == (0 if b == 2 else NC * (b - 1) - LEAD + 1):
                        sp.wait_ge(w_saved, 64)
                        sp.wait_ge(g_mm, NC * (b - 1))
                        sp.dma_start(wset[:, b % 2, W_X:W_SET].bitcast(F32), scr_w[b - 2, :, W_X:W_SET]).then_inc(wp_back, 16)
                    if t == NC * (b - 1) + 1:
                        sp.wait_ge(xp_mm, KT * NC * (b - 1))
                        sp.dma_start(wset[:, b % 2, 0:W_X].bitcast(F32), scr_w[b - 2, :, 0:W_X]).then_inc(wx_back, 16)
                if t + 1 < NP:
                    row_shift(t + 1)
                if p + 2 < NP:
                    load_x(p + 2)
                if 1 <= t and p - 1 < NP:
                    save_tp(p - 1)
                if t + 3 < NP and (t + 3) % NC == 0:
                    load_phi((t + 3) // NC)
            sp.wait_ge(stored, 16 * NP)

        @block.gpsimd
        def _(pool):
            nc.gpsimd.memset(smc(S_ONE), 1.0 / HW).then_inc(ones_set, 1)
            pool.wait_ge(ones_set, 1)
            nc.gpsimd.memset(phi4[3 * D:3 * D + 2].bitcast(F32), 1.0).then_inc(one_rows, 1)
            pool.wait_ge(one_rows, 1)
            for n in range(NP):
                b, c = divmod(n, NC)
                if c == 1:
                    pool.wait_ge(xin[(n - 1) % XRING], 16 * ((n - 1) // XRING + 1))
                    pool.wait_ge(xin[n % XRING], 16 * (n // XRING + 1))
                    if b >= 2:
                        pool.wait_ge(tsum, b - 1)
                    nc.gpsimd.tensor_tensor(acc(b), xt_in[:, (n - 1) % XRING], xt_in[:, n % XRING], ALU.add).then_inc(acc_done, 2)
                elif c in POOL_CHUNKS and c > 1:
                    pool.wait_ge(xin[n % XRING], 16 * (n // XRING + 1))
                    pool.wait_ge(acc_done, NC * b + (2 if c == 3 else c))
                    nc.gpsimd.tensor_tensor(acc(b), acc(b), xt_in[:, n % XRING], ALU.add).then_inc(acc_done, 2 if c == 3 else 1)
                elif c == DVE_CHUNKS[1]:
                    pool.wait_ge(dacc, b + 1)
                    pool.wait_ge(acc_done, NC * b + c)
                    nc.gpsimd.tensor_tensor(acc(b), acc(b), dacc_s, ALU.add).then_inc(acc_done, 1)

            def split_hi(p):
                pool.wait_ge(xst[p % XSR], 16 * (p // XSR + 1))
                nc.gpsimd.tensor_scalar(xs(p)[:, 0], xl(p), 1.0, 1.0, ALU.mult, ALU.mult).then_inc(xs_hi, 1)

            def split_lo(p):
                pool.wait_ge(xs_hi, p + 1)
                pool.wait_ge(xs_lo, p)
                nc.gpsimd.tensor_tensor(xs(p)[:, 1], xl(p), xs(p)[:, 0], ALU.subtract).then_inc(xs_lo, 1)

            def theta_hi(p):
                pool.wait_ge(th_sum, p + 1)
                wait_saved(pool, last_with_parts(p))
                nc.gpsimd.tensor_scalar(parts(p)[0], tp[0:D], 1.0, 1.0, ALU.mult, ALU.mult).then_inc(th_hi, 1)

            def theta_lo(p):
                pool.wait_ge(th_hi, p + 1)
                nc.gpsimd.tensor_tensor(parts(p)[1], tp[0:D], parts(p)[0], ALU.subtract).then_inc(th_lo, 1)

            def split_phi(p):
                pool.wait_ge(phi_pool, p + 1)
                wait_saved(pool, last_with_parts(p))
                if p >= 1:
                    pool.wait_ge(g_bias, p)
                nc.gpsimd.tensor_scalar(parts(p)[2], phip[D:2 * D], 1.0, 1.0, ALU.mult, ALU.mult).then_inc(phi_hi, 1)
                pool.wait_ge(phi_hi, p + 1)
                nc.gpsimd.tensor_tensor(parts(p)[3], phip[D:2 * D], parts(p)[2], ALU.subtract).then_inc(phi_lo, 1)
                pool.wait_ge(phi_lo, p + 1)

            def bias_g(p):
                pool.wait_ge(g_raw, p + 1)
                if p >= GPRING:
                    pool.wait_ge(gt_mm, p - GPRING + 1)
                b = p // NC
                nc.gpsimd.tensor_scalar(gpool[:, p % GPRING], graw[:], smc(S_BG + b), 0.0, ALU.add, ALU.add).then_inc(g_bias, 1)

            def probs_hi(s):
                pool.wait_ge(ex2, s + 1)
                if s >= 2:
                    pool.wait_ge(pv_mm, s - 1)
                if s == 0:
                    pool.wait_ge(w_saved, 64)
                nc.gpsimd.tensor_scalar(pT[:, s % 2, 0], expT[:, s % 2], 1.0, 1.0, ALU.mult, ALU.mult).then_inc(pt_hi, 1)

            for p in range(LEAD):
                theta_lo(p)
                split_phi(p)
                bias_g(p)
            split_hi(LEAD)
            split_lo(LEAD)
            for s in range(NS):
                t, q = divmod(s, TL)
                p = t + LEAD
                probs_hi(s)
                if q == 0 and 1 <= t and p - 1 < NP:
                    theta_hi(p - 1)
                    theta_lo(p - 1)
                if q == 1 and 1 <= t and p - 1 < NP:
                    bias_g(p - 1)
                if q == 2 and p + 1 < NP:
                    split_hi(p + 1)
                if q == 3 and p + 1 < NP:
                    split_lo(p + 1)

        @block.scalar
        def _(act):
            def gram_out(b):
                act.wait_ge(gram_mm, NC * (b + 1))
                if b >= 2:
                    act.wait_ge(mid_ev, STAGES * (b - 2) + 1)
                for m in range(KT):
                    ins = nc.scalar.activation(kk(hl_s(b))[:, m], psum[:, 4 + 2 * (b % 2) + m, 256:512], ACT.Copy, scale=1.0 / HW)
                ins.then_inc(gram_hl, 1)

            for n in range(NP):
                act.wait_ge(xin[n % XRING], 16 * (n // XRING + 1))
                if n >= XTR:
                    act.wait_ge(gram_mm, n - XTR + 1)
                nc.scalar.copy(xT(n)[:, :, 0], xt_in[:, n % XRING]).then_inc(tr_hi, 1)
                if n % NC == 1 and n > NC:
                    gram_out(n // NC - 1)
            gram_out(B - 1)

            def split_hi(p):
                act.wait_ge(xst[p % XSR], 16 * (p // XSR + 1))
                nc.scalar.copy(xs(p)[:, 0], xl(p)).then_inc(xs_hi, 1)

            def theta_hi(p):
                act.wait_ge(th_sum, p + 1)
                wait_saved(act, last_with_parts(p))
                nc.scalar.copy(parts(p)[0], tp[0:D]).then_inc(th_hi, 1)

            def y_out(t, m):
                b = t // NC
                act.wait_ge(y_mm, KT * t + m + 1)
                if m == 0 and t >= 1:
                    act.wait_ge(stored, 16 * t)
                nc.scalar.activation(ostage[:, m], psum[:, B_Y + m], ACT.Identity,
                                     bias=smc(S_FB + 2 * b + m)).then_inc(y_ev, 1)

            def theta_out(p):
                b = p // NC
                act.wait_ge(th_mm, p + 1)
                if p >= 1:
                    act.wait_ge(th_lo, p)
                    act.wait_ge(phi_pool, p)
                else:
                    act.wait_ge(bias_ev, 1)
                nc.scalar.activation(tp[:], psum[0:2 * D, theta_bank(p)], ACT.Identity,
                                     bias=smc(S_BT + b, 1, 2 * D)).then_inc(th_sum if p < LEAD else th_half, 1)

            def turned_g_hi(p):
                act.wait_ge(gt_mm, p + 1)
                nc.scalar.copy(gT[:, 0, 0, p], turned_g(p)).then_inc(gt_hi, 1)

            def weight_hi(b, half):
                act.wait_ge(w_sum, 2 * b + half + 1)
                if half == 0:
                    nc.scalar.copy(kk(wmid(b, W_TA, KT * P))[:, :, 0:2 * D], kk(t32(b))[:, :, XG:EW])
                    nc.scalar.copy(kk(wmid(b, W_GH, KT * DV)), kk(t32(b))[:, :, C:XG]).then_inc(w_hi, 1)
                else:
                    nc.scalar.copy(kk(wmid(b, W_XH, KT * C)), kk(t32(b))[:, :, 0:C]).then_inc(w_hi, 1)

            def exponent1(e):
                m, r = divmod(e, TL)
                act.wait_ge(mx, e + 1)
                if r == 0 and m >= 2:
                    act.wait_ge(ln_done, m - 1)
                nc.scalar.activation(energy_banks(e), energy_banks(e), ACT.Exp, bias=nmax[:, m % 2, r:r + 1],
                                     accum_out=den[:, m % 2, r:r + 1]).then_inc(ex1, 1)
                if r == TL - 1:
                    act.wait_ge(ex1, e + 1)
                    if m >= 1:
                        act.wait_ge(sh_all, m)
                    nc.scalar.activation(lnden[:], den[:, m % 2], ACT.Ln).then_inc(ln_done, 1)

            def exponent2(s):
                act.wait_ge(e2_mm, s + 1)
                if s >= 2:
                    act.wait_ge(pt_lo, s - 1)
                nc.scalar.activation(expT[:, s % 2], psum[:, B_E2:B_E2 + 2], ACT.Exp).then_inc(ex2, 1)

            def attn_hi(t):
                act.wait_ge(pv_mm, TL * (t + 1))
                if t >= 1:
                    act.wait_ge(y_mm, KT * t)
                else:
                    wait_saved(act, LEAD - 2)
                nc.scalar.copy(oh[:], psum[:, B_O]).then_inc(o_hi, 1)

            for p in range(EARLY_SPLITS):
                split_hi(p)
            act.wait_ge(variance, 1)
            nc.scalar.activation(smc(S_RT, 2), smc(S_VAR, 2), ACT.Sqrt).then_inc(root, 1)
            nc.scalar.add_instruction(mybir.InstLoadActFuncSet(name=nc.get_next_instruction_name(), act_func_set_id=EXP_LN_SET))
            weight_hi(0, 0)
            for p in range(LEAD):
                theta_out(p)
                theta_hi(p)
                if p == LEAD - 1:
                    for e in range(EARLIEST):
                        exponent1(e)
                for later in high_beside(p):
                    split_hi(later)
                if 2 <= p <= NC + 1:
                    turned_g_hi(p - 2)
                for b, half in weights_beside(p):
                    weight_hi(b, half)
            for e in range(EARLIEST, AHEAD - 1):
                exponent1(e)
            for s in range(NS + LAG + 4):
                t, q = divmod(s, TL)
                p = t + LEAD
                if s < NS:
                    exponent2(s)
                if s + AHEAD - 1 < NS:
                    exponent1(s + AHEAD - 1)
                if q == 0 and 2 <= t <= NP + 1:
                    y_out(t - 2, 1)
                if q == 1 and 1 <= t <= NP:
                    attn_hi(t - 1)
                if q == 2 and p < NP:
                    theta_out(p)
                if q == 3 and 1 <= t <= NP:
                    y_out(t - 1, 0)

        @block.tensor
        def _(pe):
            def split_product(o, wh, wl, vh, vl, start, stop):
                nc.tensor.matmul(o, wh, vh, start=start, stop=False)
                nc.tensor.matmul(o, wl, vh, start=False, stop=False)
                return nc.tensor.matmul(o, wh, vl, start=False, stop=stop)

            def gram(n):
                b, c = divmod(n, NC)
                pe.wait_ge(tr_lo, n + 1)
                if c == 0 and b >= 2:
                    pe.wait_ge(gram_ev, b - 1)
                for t in range(TL):
                    hl = xT(n)[:, t].rearrange("p h c -> p (h c)")
                    for m in range(KT):
                        ins = nc.tensor.matmul(psum[:, 4 + 2 * (b % 2) + m, m * P:2 * C], hl[:, m * P:(m + 1) * P],
                                               hl[:, m * P:2 * C], start=(c == 0 and t == 0), stop=(c == NC - 1 and t == TL - 1))
                ins.then_inc(gram_mm, 1)

            def image_product(b, stage):
                i = STAGES * b + stage
                o, o2 = psum[:, 2 * (i % 2)], psum[:, 2 * (i % 2) + 1]
                if i == 0:
                    pe.wait_ge(ones_set, 1)
                    pe.wait_ge(q_ev, 1)
                else:
                    pe.wait_ge(mid_ev, i)
                if stage == 0:
                    pe.wait_ge(gram_hl, b + 1)
                    hl, s1 = kk(hl_s(b)), kk(s1_s(b))
                    for m, k in ((0, 0), (0, 1), (1, 1)):
                        nc.tensor.transpose(o2[:, m * C + k * P:m * C + (k + 1) * P], hl[:, k, m * P:(m + 1) * P], ident[:])
                    pe.wait_ge(gram_ev, b + 1)
                    nc.tensor.transpose(o2[:, C:C + P], s1[:, 0, P:2 * P], ident[:])
                    pe.wait_ge(tsum, b + 1)
                    for k in range(KT):
                        ins = nc.tensor.matmul(o[:, k:k + 1], tsum_s[:, k * P:(k + 1) * P], smc(S_ONE), start=True, stop=True)
                elif stage == 1:
                    for m in range(KT):
                        for k in range(KT):
                            nc.tensor.matmul(o[:, m * P:(m + 1) * P], e_s[:, k, m * P:(m + 1) * P], wgT_s[:, k],
                                             start=(k == 0), stop=(k == KT - 1))
                    for k in range(KT):
                        ins = nc.tensor.matmul(o2[0:1, 0:P], smc(S_M + 2 * b + k), wgT_s[:, k], start=(k == 0), stop=(k == KT - 1))
                elif stage == 2:
                    for k in range(KT):
                        nc.tensor.matmul(o[:, 0:C + 1], t1_s[:, k], q_s[:, k, 0:C + 1], start=(k == 0), stop=False)
                    nc.tensor.matmul(o[:, 0:C + 1], gb_s, r_s, start=False, stop=True)
                    for m in range(KT):
                        for k in range(KT):
                            nc.tensor.matmul(o2[:, m * P:(m + 1) * P], q_s[:, k, m * P:(m + 1) * P], t1_s[:, k], start=(k == 0), stop=False)
                        ins = nc.tensor.matmul(o2[:, m * P:(m + 1) * P], r_s[:, m * P:(m + 1) * P], gb_s, start=False, stop=True)
                elif stage == 3:
                    for k in range(KT):
                        nc.tensor.matmul(o[:, 0:C + 1], vt_s[:, k], e_s[:, k, 0:C + 1], start=(k == 0), stop=(k == KT - 1))
                    for m in range(KT):
                        ins = nc.tensor.matmul(o2[:, m * C:(m + 1) * C], wwT_s[:, m * P:(m + 1) * P], v_s(b)[:, 0:C], start=True, stop=True)
                else:
                    for m, bank in ((0, o), (1, o2)):
                        ins = nc.tensor.matmul(bank[:, 0:C + 2], wwT_s[:, m * P:(m + 1) * P], ve_s, start=True, stop=True)
                ins.then_inc(mid_mm, 1)

            def theta_phi_product():
                pe.wait_ge(consts, 16 * N_CONST)
                for m in range(KT):
                    nc.tensor.matmul(psum[:, m, 0:C + 1], wp_s[:, m * P:(m + 1) * P], wtb_s, start=True, stop=True)
                nc.tensor.matmul(psum[0:1, 2, 0:C + 1], vc[:, V_BP:V_BP + 1], wtb_s, start=True, stop=True).then_inc(q_mm, 1)

            for n in range(NP):
                gram(n)
                b, c = divmod(n, NC)
                if n == NC:
                    theta_phi_product()
                if b >= 1 and 2 <= c < STAGES + 2:
                    image_product(b - 1, c - 2)
            for stage in range(STAGES):
                image_product(B - 1, stage)

            pe.wait_ge(sw_ready, 1)
            for m in range(KT):
                nc.tensor.transpose(psum[:, B_E1, m * P:(m + 1) * P], sw_s[:, m], ident[:])
            for m in range(KT):
                ins = nc.tensor.matmul(psum[:, B_E1, C:EW], sw_s[:, m], ew_s[:, m, C:EW], start=(m == 0), stop=(m == KT - 1))
            ins.then_inc(su_mm, 1)

            def bias_product():
                pe.wait_ge(d_ready, 1)
                d_v = smc(S_D, 2 * B).rearrange("p (b m) -> p b m", m=2)
                for m in range(KT):
                    nc.tensor.matmul(psum[0:2 * D, B_Y, 0:B], ew_s[:, m, XG:EW], d_v[:, :, m], start=(m == 0), stop=(m == KT - 1))
                for m in range(KT):
                    ins = nc.tensor.matmul(psum[:, B_Y, B:2 * B], ew_s[:, m, C:XG], d_v[:, :, m], start=(m == 0), stop=(m == KT - 1))
                ins.then_inc(bias_mm, 1)

            def weight_product(b, half):
                if b == 0 and half == 0:
                    pe.wait_ge(su_ev, 1)
                elif b > 0:
                    pe.wait_ge(w_sum, 2 * b + half - 1)
                cols = half_columns(half)
                for m in range(KT):
                    ins = nc.tensor.matmul(psum[:, half_banks(half) + m, cols], v_s(b)[:, m * P:(m + 1) * P], su_s[:, cols], start=True, stop=True)
                ins.then_inc(w_mm, 1)

            def project_theta(p, shifts=0):
                b = p // NC
                pe.wait_ge(xs_lo, p + 1)
                if p % NC == 0:
                    if b < 2:
                        pe.wait_ge(w_lo, 2 * b + 1)
                    else:
                        pe.wait_ge(wp_back, 16 * (b - 1))
                if p >= LEAD:
                    pe.wait_ge(sh_ev, shifts)
                elif p >= 2:
                    pe.wait_ge(th_sum, p - 1)
                o, w, x = psum[:, theta_bank(p)], wset[:, b % 2], xs(p)
                for k in range(KT):
                    if p < LEAD:
                        ta = w[:, W_TA + k * P:W_TA + (k + 1) * P]
                        ins = split_product(o[0:2 * D], ta[:, 0:2 * D], ta[:, 2 * D:4 * D], x[:, 0, k], x[:, 1, k], k == 0, k == KT - 1)
                        continue
                    nc.tensor.matmul(o, w[:, W_TA + k * P:W_TA + (k + 1) * P], x[:, 0, k], start=(k == 0), stop=False)
                    ins = nc.tensor.matmul(o, w[:, W_TB + k * P:W_TB + (k + 1) * P], x[:, 1, k], start=False, stop=(k == KT - 1))
                ins.then_inc(th_mm, 1)

            def project_g(p):
                b = p // NC
                if p >= LEAD:
                    pe.wait_ge(th_sum, p + 1)
                elif p >= 1:
                    pe.wait_ge(g_raw, p)
                else:
                    pe.wait_ge(bias_ev, 1)
                o, w, x = psum[:, g_bank(p)], wset[:, b % 2], xs(p)
                for k in range(KT):
                    ins = split_product(o, w[:, W_GH + k * DV:W_GH + (k + 1) * DV], w[:, W_GL + k * DV:W_GL + (k + 1) * DV],
                                        x[:, 0, k], x[:, 1, k], k == 0, k == KT - 1)
                ins.then_inc(g_mm, 1)

            def turn_g(p, gs, shifts):
                pe.wait_ge(g_bias, p + 1)
                if p >= 1:
                    pe.wait_ge(gt_lo, p)
                if gs > 0:
                    pe.wait_ge(g_raw, gs)
                if shifts > 0:
                    pe.wait_ge(sh_ev, shifts)
                nc.tensor.transpose(turned_g(p), gpool[:, p % GPRING], ident[:]).then_inc(gt_mm, 1)

            def turn_shift(m, turned, gs):
                pe.wait_ge(sh_two, m + 1)
                pe.wait_ge(gt_lo, turned)
                if gs > 0:
                    pe.wait_ge(g_raw, gs)
                if m >= 1:
                    pe.wait_ge(sh_ev, m)
                nc.tensor.transpose(turned_shift(m), shift2[:].rearrange("p h r -> p (h r)"), ident[:]).then_inc(sh_mm, 1)

            def energies1(e):
                m, r = divmod(e, TL)
                b = m // NC
                if r == 0:
                    pe.wait_ge(th4[m % TH4], 32 * (m // TH4 + 1))
                    if m % NC == 0:
                        pe.wait_ge(ph4, 48 * (b + 1))
                if e >= AHEAD:
                    pe.wait_ge(ex1, e)
                elif e >= 3:
                    pe.wait_ge(ex1, e - 1 if e == AHEAD - 1 else e - 2)
                elif e == 2:
                    pe.wait_ge(th_sum, LEAD)
                else:
                    pe.wait_ge(w_sum, 2 * B)
                for h in range(2):
                    ins = nc.tensor.matmul(energy_banks(e)[:, h], theta4[0:3 * D, m % TH4, r * P:(r + 1) * P],
                                           phi4[0:3 * D, b % 2, h * CH:(h + 1) * CH], start=True, stop=True)
                ins.then_inc(e1_mm, 1)

            def energies2(s):
                t, q = divmod(s, TL)
                b = t // NC
                if q == 0:
                    pe.wait_ge(sh_row[t % TH4], 16 * (t // TH4 + 1))
                if s >= 1:
                    pe.wait_ge(ex2, s)
                else:
                    pe.wait_ge(one_rows, 1)
                    pe.wait_ge(ex1, AHEAD - 1)
                    pe.wait_ge(th_sum, LEAD)
                    pe.wait_ge(g_raw, LEAD)
                for jj in range(2):
                    ins = nc.tensor.matmul(psum[:, B_E2 + jj], phi4[0:3 * D + 2, b % 2, (2 * q + jj) * P:(2 * q + jj + 1) * P],
                                           theta4[0:3 * D + 2, t % TH4], start=True, stop=True)
                ins.then_inc(e2_mm, 1)

            def attend(s):
                t, q = divmod(s, TL)
                b = t // NC
                pe.wait_ge(pt_lo, s + 1)
                if q == 0:
                    if t >= 1:
                        pe.wait_ge(o_lo, t)
                    if t % NC == 0:
                        pe.wait_ge(gt_lo, NC * (b + 1))
                for jj in range(2):
                    ins = split_product(psum[:, B_O], gT[:, b % 2, 0, 2 * q + jj], gT[:, b % 2, 1, 2 * q + jj],
                                        pT[:, s % 2, 0, jj], pT[:, s % 2, 1, jj],
                                        q == 0 and jj == 0, q == TL - 1 and jj == 1)
                ins.then_inc(pv_mm, 1)

            def x1_part(t, m):
                b = t // NC
                if t % NC == 0 and m == 0:
                    if b < 2:
                        pe.wait_ge(w_lo, 2 * b + 2)
                    else:
                        pe.wait_ge(wx_back, 16 * (b - 1))
                if t >= 1:
                    pe.wait_ge(y_ev, KT * (t - 1) + m + 1)
                w, x = wset[:, b % 2], xs(t)
                for k in range(KT):
                    cols = slice(k * C + m * P, k * C + (m + 1) * P)
                    ins = split_product(psum[:, B_Y + m], w[:, W_XH:W_XL][:, cols], w[:, W_XL:W_GH][:, cols],
                                        x[:, 0, k], x[:, 1, k], k == 0, False)
                ins.then_inc(xp_mm, 1)

            def convolve(t, m):
                pe.wait_ge(o_lo, t + 1)
                if t == 0 and m == 0:
                    pe.wait_ge(wo_done, 1)
                split_product(psum[:, B_Y + m], woh[:, m * P:(m + 1) * P], wol[:, m * P:(m + 1) * P], oh[:], ol[:],
                              False, True).then_inc(y_mm, 1)

            weight_product(0, 0)
            bias_product()
            for p in range(LEAD):
                project_theta(p)
                if p == LEAD - 1:
                    for e in range(EARLIEST):
                        energies1(e)
                project_g(p)
                if 2 <= p <= NC + 1:
                    turn_g(p - 2, 0, 0)
                for b, half in weights_beside(p):
                    weight_product(b, half)
            for e in range(EARLIEST, AHEAD):
                energies1(e)
                if e == TL + 1:
                    turn_shift(0, NC, 0)
            for s in range(NS + LAG + 3):
                t, q = divmod(s, TL)
                p = t + LEAD
                if s < NS:
                    energies2(s)
                if q in (0, 1) and 1 <= t <= NP:
                    x1_part(t - 1, q)
                if q == 2 and p < NP:
                    project_theta(p, t + 2)
                if q == 3 and 1 <= t <= NP:
                    convolve(t - 1, 1)
                if LAG <= s < NS + LAG:
                    attend(s - LAG)
                if q == 0 and 1 <= t and t + NC - 1 < NP:
                    turn_g(t + NC - 1, min(p, NP), t + 1)
                if q == 1 and t + 1 < NP:
                    turn_shift(t + 1, min(t + NC, NP), min(p, NP))
                if q == 2 and 1 <= t <= NP:
                    convolve(t - 1, 0)
                if q == 3 and p < NP:
                    project_g(p)
                if s + AHEAD < NS:
                    energies1(s + AHEAD)

        @block.vector
        def _(dve):
            tt, ts, stt, cp = nc.vector.tensor_tensor, nc.vector.tensor_scalar, nc.vector.scalar_tensor_tensor, nc.vector.tensor_copy
            steps = [0]

            def then(ins):
                steps[0] += 1
                ins.then_inc(chain, 1)
                dve.wait_ge(chain, steps[0])

            def gram_sum(b):
                dve.wait_ge(gram_hl, b + 1)
                s1, hl, o = kk(s1_s(b)), kk(hl_s(b)), psum[:, 4 + 2 * (b % 2):6 + 2 * (b % 2)]
                stt(s1[:, 0], o[:, 0, 0:C], 1.0 / HW, hl[:, 0], ALU.mult, ALU.add)
                stt(s1[:, 1, P:C], o[:, 1, P:C], 1.0 / HW, hl[:, 1, P:C], ALU.mult, ALU.add)
                cp(s1[:, 1, 0:P], hl[:, 1, 0:P]).then_inc(gram_ev, 1)

            def pixel_sum(b):
                dve.wait_ge(acc_done, NC * (b + 1))
                if b >= 1:
                    dve.wait_ge(mid_mm, STAGES * (b - 1) + 1)
                nc.vector.tensor_reduce(tsum_s, acc(b).rearrange("p t c -> p c t"), AX.X, ALU.add).then_inc(tsum, 1)

            def image_result(b, stage):
                i = STAGES * b + stage
                o, o2 = psum[:, 2 * (i % 2)], psum[:, 2 * (i % 2) + 1]
                dve.wait_ge(mid_mm, i + 1)
                if stage == 0:
                    cp(e_s[:, :, C], o[:, 0:2])
                    cp(smc(S_M + 2 * b, 2), o[:, 0:2])
                    ins = tt(e_s[:, :, 0:C], kk(o2), kk(s1_s(b)), ALU.add)
                elif stage == 1:
                    for m in range(KT):
                        stt(t1_s[:, m], bgB_s, smc(S_M + 2 * b + m), o[:, m * P:(m + 1) * P], ALU.mult, ALU.add)
                    ins = tt(gb_s, o2[0:1, 0:P], bgB_s[0:1], ALU.add)
                elif stage == 2:
                    cp(mid(O_VT, C), o2[:, 0:C])
                    ins = cp(v_s(b), o[:, 0:C + 1])
                elif stage == 3:
                    cp(ve_s[:, 0:C + 1], o[:, 0:C + 1])
                    cp(ve_s[:, C + 1:C + 2], v_s(b)[:, C:C + 1])
                    ins = cp(mid(O_A, KT * C), o2)
                else:
                    for m, bank in ((0, o), (1, o2)):
                        col = S_CW + 4 * b + 2 * m
                        cp(smc(col), bank[:, C:C + 1])
                        ts(smc(col + 1), bank[:, C + 1:C + 2], vc[:, V_WB + m:V_WB + m + 1], None, ALU.add)
                        ins = nc.vector.tensor_tensor_reduce(out=mid(O_JUNK + m * C, C), in0=bank[:, 0:C], in1=a_s[:, m], scale=1.0,
                                                             scalar=0.0, op0=ALU.mult, op1=ALU.add, accum_out=smc(S_Q + 2 * b + m))
                ins.then_inc(mid_ev, 1)

            for n in range(NP):
                b, c = divmod(n, NC)
                dve.wait_ge(tr_hi, n + 1)
                tt(xT(n)[:, :, 1], xt_in[:, n % XRING], xT(n)[:, :, 0], ALU.subtract).then_inc(tr_lo, 1)
                if n == NC:
                    dve.wait_ge(q_mm, 1)
                    cp(q_s[:, :, 0:C + 1], psum[:, 0:2, 0:C + 1])
                    cp(r_s, psum[0:1, 2, 0:C + 1]).then_inc(q_ev, 1)
                if b >= 2 and c == 0:
                    image_result(b - 2, STAGES - 1)
                if b >= 1 and c == 1:
                    gram_sum(b - 1)
                    pixel_sum(b - 1)
                if b >= 1 and 4 <= c < STAGES + 3:
                    image_result(b - 1, c - 4)
                if c == DVE_CHUNKS[1]:
                    m = n - DVE_CHUNKS[1] + DVE_CHUNKS[0]
                    if b >= 1:
                        dve.wait_ge(acc_done, NC * (b - 1) + DVE_CHUNKS[1] + 1)
                    tt(dacc_s, xt_in[:, m % XRING], xt_in[:, n % XRING], ALU.add).then_inc(dacc, 1)
            image_result(B - 2, STAGES - 1)
            pixel_sum(B - 1)
            gram_sum(B - 1)

            def split_x(p):
                dve.wait_ge(xs_hi, p + 1)
                tt(xs(p)[:, 1], xl(p), xs(p)[:, 0], ALU.subtract).then_inc(xs_lo, 1)

            for stage in range(STAGES):
                image_result(B - 1, stage)
                if stage < STAGES - 1:
                    split_x(stage)

            def per_image(off, m):
                return sm[:, off:off + 2 * B].rearrange("p (b m) -> p b m", m=2)[:, :, m]

            def all_images(off):
                return smc(off, 2 * B).rearrange("p (b m) -> p b m", m=2)

            cw = smc(S_CW, 4 * B).rearrange("p (b m j) -> p b m j", m=2, j=2)
            dve.wait_ge(mid_ev, STAGES * B)
            tt(all_images(S_U), cw[:, :, :, 0], cw[:, :, :, 1], ALU.add)
            then(tt(all_images(S_AM), cw[:, :, :, 0], cw[:, :, :, 0], ALU.mult))
            nc.vector.tensor_reduce(smc(S_MU, 2), smc(S_U, 8).rearrange("p (b m) -> p m b", m=2), AX.X, ALU.add)
            then(tt(smc(S_Q, 8), smc(S_Q, 8), smc(S_AM, 8), ALU.subtract))
            then(ts(smc(S_MU, 2), smc(S_MU, 2), 1.0 / B, None, ALU.mult))
            for m in range(KT):
                ins = ts(per_image(S_DEV, m), per_image(S_U, m), smc(S_MU + m), None, ALU.subtract)
            then(ins)
            then(tt(smc(S_DEV, 8), smc(S_DEV, 8), smc(S_DEV, 8), ALU.mult))
            then(tt(smc(S_DEV, 8), smc(S_DEV, 8), smc(S_Q, 8), ALU.add))
            then(nc.vector.tensor_reduce(smc(S_VAR, 2), smc(S_DEV, 8).rearrange("p (b m) -> p m b", m=2), AX.X, ALU.add))
            ts(smc(S_VAR, 2), smc(S_VAR, 2), 1.0 / B, BN_EPS, ALU.mult, ALU.add).then_inc(variance, 1)
            dve.wait_ge(root, 1)
            v, r, h = smc(S_VAR, 2), smc(S_S, 2), smc(S_DEV, 2)
            then(nc.vector.reciprocal(r, smc(S_RT, 2)))
            then(tt(h, r, r, ALU.mult))
            then(tt(h, h, v, ALU.mult))
            then(ts(h, h, -0.5, 1.5, ALU.mult, ALU.add))
            then(tt(r, r, h, ALU.mult))
            then(tt(r, r, vc[:, V_GAM:V_GAM + 2], ALU.mult))
            for m in range(KT):
                ins = ts(sw_s[:, m], ww_s[:, m], smc(S_S + m), None, ALU.mult)
            ins.then_inc(sw_ready, 1)
            for m in range(KT):
                ins = ts(per_image(S_D, m), cw[:, :, m, 1], smc(S_MU + m), smc(S_S + m), ALU.subtract, ALU.mult)
            then(ins)
            for m in range(KT):
                ins = ts(per_image(S_D, m), per_image(S_D, m), vc[:, V_BETA + m:V_BETA + m + 1], None, ALU.add)
            ins.then_inc(d_ready, 1)
            dve.wait_ge(d_ready, 1)
            then(ts(smc(S_GB, 2), vc[:, V_BO:V_BO + 2], vc[:, V_G:V_G + 1], None, ALU.mult))
            for m in range(KT):
                ts(per_image(S_FB, m), per_image(S_D, m), smc(S_GB + m), None, ALU.add)
            dve.wait_ge(su_mm, 1)
            cp(su_s, psum[:, B_E1, 0:EW]).then_inc(su_ev, 1)

            def weight_sum(b, half):
                dve.wait_ge(w_mm, 2 * b + half + 1)
                cols = half_columns(half)
                tt(kk(t32(b))[:, :, cols], psum[:, half_banks(half):half_banks(half) + 2, cols], ew_s[:, :, cols], ALU.add).then_inc(w_sum, 1)

            def weight_lo(b, half):
                dve.wait_ge(w_hi, 2 * b + half + 1)
                if half == 0:
                    ta, tb = kk(wmid(b, W_TA, KT * P)), kk(wmid(b, W_TB, KT * P))
                    ts(tb[:, :, 0:2 * D], kk(ident[:]), 0.0, None, ALU.mult)
                    cp(tb[:, :, 2 * D:4 * D], kk(t32(b))[:, :, XG:EW])
                    tt(ta[:, :, 2 * D:4 * D], kk(t32(b))[:, :, XG:EW], ta[:, :, 0:2 * D], ALU.subtract)
                    tt(kk(wmid(b, W_GL, KT * DV)), kk(t32(b))[:, :, C:XG], kk(wmid(b, W_GH, KT * DV)), ALU.subtract).then_inc(w_lo, 1)
                else:
                    tt(kk(wmid(b, W_XL, KT * C)), kk(t32(b))[:, :, 0:C], kk(wmid(b, W_XH, KT * C)), ALU.subtract).then_inc(w_lo, 1)

            split_x(STAGES - 1)
            weight_sum(0, 0)
            weight_lo(0, 0)
            dve.wait_ge(bias_mm, 1)
            ts(smc(S_BT, B, 2 * D), psum[0:2 * D, B_Y, 0:B], vc[0:2 * D, V_BTP:V_BTP + 1], None, ALU.add)
            ts(smc(S_BG, B), psum[:, B_Y, B:2 * B], vc[:, V_BG:V_BG + 1], None, ALU.add).then_inc(bias_ev, 1)
            then(ts(mid(O_GWO, C), wo_s, vc[:, V_G:V_G + 1], None, ALU.mult))
            then(cp(woh[:], mid(O_GWO, C)))
            tt(wol[:], mid(O_GWO, C), woh[:], ALU.subtract).then_inc(wo_done, 1)
            split_x(STAGES)

            def theta_sum(p):
                dve.wait_ge(th_half, p - LEAD + 1)
                tt(tp[:], psum[2 * D:4 * D, theta_bank(p)], tp[:], ALU.add).then_inc(th_sum, 1)

            def phi_out(p):
                dve.wait_ge(th_sum, p + 1)
                if p >= 1:
                    dve.wait_ge(phi_lo, p)
                    if p >= LEAD:
                        wait_saved(dve, last_with_parts(p))
                nc.vector.tensor_reduce(phip[D:2 * D].rearrange("p (r c) -> p r c", c=W_IMG // 2),
                                        tp[D:2 * D].rearrange("p (r i c j) -> p r c i j", i=2, j=2, c=W_IMG // 2),
                                        AX.XY, ALU.max).then_inc(phi_pool, 1)
                if p < LEAD:
                    return
                dve.wait_ge(phi_pool, p + 1)
                cp(phh[D:2 * D], phip[D:2 * D]).then_inc(phi_hi, 1)
                dve.wait_ge(phi_hi, p + 1)
                tt(phl[D:2 * D], phip[D:2 * D], phh[D:2 * D], ALU.subtract).then_inc(phi_lo, 1)

            def pool_g(p):
                dve.wait_ge(g_mm, p + 1)
                if p >= 1:
                    dve.wait_ge(g_bias, p)
                nc.vector.tensor_reduce(graw[:].rearrange("p (r c) -> p r c", c=W_IMG // 2),
                                        psum[:, g_bank(p)].rearrange("p (r i c j) -> p r c i j", i=2, j=2, c=W_IMG // 2),
                                        AX.XY, ALU.max).then_inc(g_raw, 1)

            def split_g(p):
                b, c = divmod(p, NC)
                dve.wait_ge(gt_mm, p + 1)
                if b >= 2:
                    dve.wait_ge(pv_mm, TL * NC * (b - 1))
                if p >= NC:
                    cp(gT[:, b % 2, 0, c], turned_g(p)).then_inc(gt_hi, 1)
                dve.wait_ge(gt_hi, p + 1)
                tt(gT[:, b % 2, 1, c], turned_g(p), gT[:, b % 2, 0, c], ALU.subtract).then_inc(gt_lo, 1)

            def row_max(e):
                m, r = divmod(e, TL)
                dve.wait_ge(e1_mm, e + 1)
                if m >= 2 and r == 0:
                    dve.wait_ge(ex1, TL * (m - 1))
                    dve.wait_ge(sh_all, m - 1)
                nc.vector.tensor_reduce(nmax[:, m % 2, r:r + 1], energy_banks(e), AX.XY, ALU.max, negate=True).then_inc(mx, 1)

            def make_shift(m):
                dve.wait_ge(ln_done, m + 1)
                tt(shift[:], nmax[:, m % 2], lnden[:], ALU.subtract).then_inc(sh_all, 1)
                dve.wait_ge(sh_all, m + 1)
                cp(shift_r[:], shift[:]).then_inc(sh_hi, 1)
                dve.wait_ge(sh_hi, m + 1)
                if m >= 1:
                    dve.wait_ge(sh_mm, m)
                cp(shift2[:, 0], shift_r[:])
                tt(shift2[:, 1], shift[:], shift_r[:], ALU.subtract).then_inc(sh_two, 1)

            def shift_out(m):
                dve.wait_ge(sh_mm, m + 1)
                if m >= 1:
                    dve.wait_ge(sh_saved, 16 * m)
                cp(shiftT[:], turned_shift(m)).then_inc(sh_ev, 1)

            def probs_lo(s):
                dve.wait_ge(pt_hi, s + 1)
                tt(pT[:, s % 2, 1], expT[:, s % 2], pT[:, s % 2, 0], ALU.subtract).then_inc(pt_lo, 1)

            def attn_lo(t):
                dve.wait_ge(o_hi, t + 1)
                tt(ol[:], psum[:, B_O], oh[:], ALU.subtract).then_inc(o_lo, 1)

            for p in range(LEAD):
                phi_out(p)
                for later in low_beside(p):
                    split_x(later)
                if p == LEAD - 1:
                    for e in range(EARLIEST):
                        row_max(e)
                pool_g(p)
                if 2 <= p <= NC + 1:
                    split_g(p - 2)
                for b, half in weights_beside(p):
                    weight_sum(b, half)
                for b, half in weights_beside(p):
                    weight_lo(b, half)
            for e in range(EARLIEST, AHEAD - 1):
                row_max(e)
                if e == TL:
                    make_shift(0)
                if e == TL + 1:
                    shift_out(0)
            for s in range(NS + LAG + 2):
                t, q = divmod(s, TL)
                p = t + LEAD
                if s + AHEAD - 1 < NS:
                    row_max(s + AHEAD - 1)
                if q == 0 and 1 <= t and p - 1 < NP:
                    pool_g(p - 1)
                if q == 3 and p < NP:
                    theta_sum(p)
                if 1 <= s <= NS:
                    probs_lo(s - 1)
                if q == 0 and 1 <= t and t + NC - 1 < NP:
                    split_g(t + NC - 1)
                if q == 0 and t + 1 < NP:
                    make_shift(t + 1)
                if q == 1 and t + 1 < NP:
                    shift_out(t + 1)
                if q == 1 and 1 <= t <= NP:
                    attn_lo(t - 1)
                if q == 2 and 1 <= t and p - 1 < NP:
                    phi_out(p - 1)


def kernel(**inputs):
    import numpy as np
    import concourse.bacc as bacc
    from concourse.bass_utils import run_bass_kernel_spmd

    def a(name):
        return np.asarray(inputs[name])

    def tiles(w):
        return np.ascontiguousarray(w.reshape(KT, P, -1).transpose(1, 0, 2).reshape(P, -1))

    def col(v):
        return tiles(v.reshape(-1, 1)) if v.size == C else v.reshape(-1, 1)

    xin = a("x").reshape(B, C, HW)
    f = xin.dtype
    btp = np.zeros((P, 1), f)
    btp[0:D, 0] = a("L1_conv_theta_b")
    btp[D:2 * D, 0] = a("L1_conv_phi_b")
    w1T = np.concatenate([a("L1_conv_g_w"), a("L1_conv_theta_w"), a("L1_conv_phi_w")]).T
    arrays = {
        "xT": np.ascontiguousarray(xin.transpose(0, 2, 1)),
        "x": xin,
        "wp": a("L0_conv_phi_w"),
        "wgT": tiles(a("L0_conv_g_w").T),
        "wtb": np.concatenate([a("L0_conv_theta_w"), a("L0_conv_theta_b").reshape(-1, 1)], 1),
        "wwT": np.ascontiguousarray(a("L0_conv_w_w").T),
        "ww": tiles(a("L0_conv_w_w")),
        "ew": tiles(np.concatenate([np.eye(C, dtype=f), w1T], 1)),
        "woT": np.ascontiguousarray(a("L1_conv_out_w").T),
        "bgB": np.repeat(a("L0_conv_g_b").reshape(1, P), P, 0),
        "cols": np.ascontiguousarray(np.concatenate(
            [col(a("L0_conv_w_b")), col(a("L0_conv_gamma")), col(a("L0_conv_beta")),
             col(a("L1_conv_out_b")), btp, col(a("L1_conv_g_b")), np.repeat(a("L1_conv_gamma").reshape(1, 1), P, 0),
             col(a("L0_conv_phi_b"))], 1)),
        "eye": np.eye(P, dtype=f),
    }
    nc = bacc.Bacc("TRN2", target_bir_lowering=False, num_devices=1)
    args = [nc.dram_tensor("in_" + n, v.shape, mybir.dt.from_np(v.dtype), kind="ExternalInput").ap() for n, v in arrays.items()]
    out = nc.dram_tensor("out_y", (B, C, HW), F32, kind="ExternalOutput").ap()
    nonlocal_then_attention(nc, *args, out)
    r = run_bass_kernel_spmd(nc, [{"in_" + n: np.ascontiguousarray(v) for n, v in arrays.items()}], core_ids=[0])
    return r.results[0]["out_y"].reshape(B, C, 64, 64)
```
